# Optimizing a Trainium2 kernel written in Bass

```python
import numpy as np
import jax
import jax.numpy as jnp

def _softmax(x, axis=-1):
    return jax.nn.softmax(x, axis=axis)

def _gelu(x):
    return jax.nn.gelu(x, approximate=True)

def _silu(x):
    return jax.nn.silu(x)

def _sigmoid(x):
    return jax.nn.sigmoid(x)

def _layernorm(x, axis=-1, eps=1e-05):
    m = jnp.mean(x, axis=axis, keepdims=True)
    v = jnp.var(x, axis=axis, keepdims=True)
    return (x - m) / jnp.sqrt(v + eps)

def _scatter_add(tgt, idx, src, axis=0):
    return tgt.at[idx].add(src)

def _segment_sum(src, seg, n):
    return jax.ops.segment_sum(src, seg, n)
kernel_name = 'mk_sandwich_d1_jaxref_r8_2b6a85'

def setup_inputs(seed: int=0):
    np.random.seed(seed)
    _w = jnp.asarray

    def _L0_attn_setup():
        import jax, jax.numpy as jnp
        import numpy as np
        B, S, D = (2, 512, 256)
        LN_EPS = 1e-05
        key = jax.random.key(seed)
        ks = jax.random.split(key, 4)
        s = 0.02
        return {'hidden_states': jax.random.normal(ks[0], (B, S, D), jnp.float32), 'attention_mask': jnp.ones((B, S), jnp.int32), 'ln_g': jnp.ones((D,), jnp.float32), 'ln_b': jnp.zeros((D,), jnp.float32), 'Wq': jax.random.normal(ks[1], (D, D), jnp.float32) * s, 'bq': jnp.zeros((D,), jnp.float32), 'Wqa': jnp.zeros((D, D), jnp.float32), 'bqa': jnp.ones((D,), jnp.float32), 'Wk': jax.random.normal(ks[2], (D, D), jnp.float32) * s, 'bk': jnp.zeros((D,), jnp.float32), 'Wka': jnp.zeros((D, D), jnp.float32), 'bka': jnp.ones((D,), jnp.float32), 'Wv': jax.random.normal(ks[3], (D, D), jnp.float32) * s, 'bv': jnp.zeros((D,), jnp.float32)}
    _L0_attn_in = _L0_attn_setup()

    def _L0_ffn_setup():
        import jax, jax.numpy as jnp
        import numpy as np
        TOPK = 2
        NORM_TOPK = True
        SCALE = 1.0
        EPS = 1e-09
        key = jax.random.key(seed)
        ks = jax.random.split(key, 9)
        h, i, E = (256, 128, 16)
        std = 0.02
        return {'x': jax.random.normal(ks[0], (1, 256, h), jnp.float32), 'Wr': jax.random.normal(ks[1], (E, h), jnp.float32) * std, 'bias': jnp.zeros((E,), jnp.float32), 'Wg': jax.random.normal(ks[2], (E, h, i), jnp.float32) * std, 'Wu': jax.random.normal(ks[3], (E, h, i), jnp.float32) * std, 'Wd': jax.random.normal(ks[4], (E, i, h), jnp.float32) * std, 'sWg': jax.random.normal(ks[5], (h, i), jnp.float32) * std, 'sWu': jax.random.normal(ks[6], (h, i), jnp.float32) * std, 'sWd': jax.random.normal(ks[7], (i, h), jnp.float32) * std}
    _L0_ffn_in = _L0_ffn_setup()
    _d = {'L0_attn_hidden_states': _L0_attn_in['hidden_states'], 'L0_attn_attention_mask': _L0_attn_in['attention_mask'], 'L0_attn_ln_g': _L0_attn_in['ln_g'], 'L0_attn_ln_b': _L0_attn_in['ln_b'], 'L0_attn_Wq': _L0_attn_in['Wq'], 'L0_attn_bq': _L0_attn_in['bq'], 'L0_attn_Wqa': _L0_attn_in['Wqa'], 'L0_attn_bqa': _L0_attn_in['bqa'], 'L0_attn_Wk': _L0_attn_in['Wk'], 'L0_attn_bk': _L0_attn_in['bk'], 'L0_attn_Wka': _L0_attn_in['Wka'], 'L0_attn_bka': _L0_attn_in['bka'], 'L0_attn_Wv': _L0_attn_in['Wv'], 'L0_attn_bv': _L0_attn_in['bv'], 'L0_ffn_Wr': _L0_ffn_in['Wr'], 'L0_ffn_bias': _L0_ffn_in['bias'], 'L0_ffn_Wg': _L0_ffn_in['Wg'], 'L0_ffn_Wu': _L0_ffn_in['Wu'], 'L0_ffn_Wd': _L0_ffn_in['Wd'], 'L0_ffn_sWg': _L0_ffn_in['sWg'], 'L0_ffn_sWu': _L0_ffn_in['sWu'], 'L0_ffn_sWd': _L0_ffn_in['sWd']}
    _x0 = _d['L0_attn_hidden_states']
    _d['L0_attn_hidden_states'] = jax.random.normal(jax.random.fold_in(jax.random.key(seed), 1), (2, 512, 256), dtype=_x0.dtype)
    del _x0
    return _d

def reference(L0_attn_hidden_states, L0_attn_attention_mask, L0_attn_ln_g, L0_attn_ln_b, L0_attn_Wq, L0_attn_bq, L0_attn_Wqa, L0_attn_bqa, L0_attn_Wk, L0_attn_bk, L0_attn_Wka, L0_attn_bka, L0_attn_Wv, L0_attn_bv, L0_ffn_Wr, L0_ffn_bias, L0_ffn_Wg, L0_ffn_Wu, L0_ffn_Wd, L0_ffn_sWg, L0_ffn_sWu, L0_ffn_sWd):

    def _L0_attn_ref(hidden_states, attention_mask, ln_g, ln_b, Wq, bq, Wqa, bqa, Wk, bk, Wka, bka, Wv, bv):
        import jax, jax.numpy as jnp
        import numpy as np
        B, S, D = (2, 512, 256)
        LN_EPS = 1e-05
        mu = jnp.mean(hidden_states, axis=-1, keepdims=True)
        var = jnp.var(hidden_states, axis=-1, keepdims=True)
        h = (hidden_states - mu) * jax.lax.rsqrt(var + LN_EPS) * ln_g + ln_b
        lin = lambda x, W, b: x @ W.T + b
        scale = 1.0 / jnp.sqrt(jnp.float32(D))
        query = lin(h, Wq, bq)
        keys = lin(h, Wk, bk)
        values = lin(h, Wv, bv)
        qw = jnp.exp(lin(query, Wqa, bqa) * scale)
        qw = qw / jnp.cumsum(qw, axis=1)
        pooled_query = jnp.cumsum(qw * query, axis=1)
        mixed_keys = pooled_query * keys
        kw = jnp.exp(lin(mixed_keys, Wka, bka) * scale)
        kw = kw / jnp.cumsum(kw, axis=1)
        pooled_keys = jnp.cumsum(kw * mixed_keys, axis=1)
        return pooled_keys * values

    def _L0_ffn_ref(x, Wr, bias, Wg, Wu, Wd, sWg, sWu, sWd):
        import jax, jax.numpy as jnp
        import numpy as np
        TOPK = 2
        NORM_TOPK = True
        SCALE = 1.0
        EPS = 1e-09
        b, s, h = x.shape
        E = Wr.shape[0]
        xt = x.reshape(b * s, h)
        logits = xt @ Wr.T + bias
        probs = jax.nn.softmax(logits, axis=-1)
        topk_val, topk_idx = jax.lax.top_k(probs, TOPK)
        if NORM_TOPK:
            w = topk_val / (jnp.sum(topk_val, axis=-1, keepdims=True) + EPS)
        else:
            w = topk_val
        w = w * SCALE
        g = jnp.einsum('th,ehi->tei', xt, Wg)
        u = jnp.einsum('th,ehi->tei', xt, Wu)
        y = jnp.einsum('tei,eih->teh', jax.nn.silu(g) * u, Wd)
        oh = jax.nn.one_hot(topk_idx, E, dtype=x.dtype)
        routed = jnp.einsum('tke,tk,teh->th', oh, w, y)
        shared = jax.nn.silu(xt @ sWg) * (xt @ sWu) @ sWd
        return (routed + shared).reshape(b, s, h)
    x = L0_attn_hidden_states
    x = x + _layernorm(_L0_attn_ref(_layernorm(x, axis=-1), L0_attn_attention_mask, L0_attn_ln_g, L0_attn_ln_b, L0_attn_Wq, L0_attn_bq, L0_attn_Wqa, L0_attn_bqa, L0_attn_Wk, L0_attn_bk, L0_attn_Wka, L0_attn_bka, L0_attn_Wv, L0_attn_bv), axis=-1)
    x = x + _layernorm(_L0_ffn_ref(_layernorm(x, axis=-1), L0_ffn_Wr, L0_ffn_bias, L0_ffn_Wg, L0_ffn_Wu, L0_ffn_Wd, L0_ffn_sWg, L0_ffn_sWu, L0_ffn_sWd), axis=-1)
    return x

_drawn_inputs = setup_inputs


def setup_inputs(seed=0):
    import zlib

    import numpy as np

    out = dict(_drawn_inputs(seed))
    spreads = {'L0_attn_ln_g': (1.0, 0.2),
     'L0_attn_ln_b': (0.0, 0.1),
     'L0_attn_bq': (0.0, 0.1),
     'L0_attn_Wqa': (0.0, 0.1),
     'L0_attn_bqa': (1.0, 0.2),
     'L0_attn_bk': (0.0, 0.1),
     'L0_attn_Wka': (0.0, 0.1),
     'L0_attn_bka': (1.0, 0.2),
     'L0_attn_bv': (0.0, 0.1),
     'L0_ffn_bias': (0.0, 0.1)}
    factors = {}
    for name, (base, spread) in spreads.items():
        noise = np.random.default_rng([zlib.crc32(name.encode()), seed]).standard_normal(out[name].shape)
        drawn = base * np.exp(spread * noise) if base else spread * noise
        out[name] = jnp.asarray(drawn.astype(out[name].dtype))
    for name, factor in factors.items():
        out[name] = (out[name] * factor).astype(out[name].dtype)
    return out
```

```python
from contextlib import ExitStack

import concourse.bass as bass
from concourse import mybir

F32 = mybir.dt.float32
F32R = mybir.dt.float32r
BF16 = mybir.dt.bfloat16
I32 = mybir.dt.int32
U32 = mybir.dt.uint32
ALU = mybir.AluOpType
ACT = mybir.ActivationFunctionType
AX_X = mybir.AxisListType.X

P = 128
LN_EPS = 1e-5
TOPK_EPS = 1e-9


def block_kernel(nc, x, attn_w, misc, expert_w, out):
    B, S, D = x.shape
    T = B * S
    C = D // P
    NJ = T // P
    JB = S // P
    _, NX, EW = expert_w.shape
    E = NX - 1
    GU = 2 * P
    NCOL = 7
    K = 2
    TILES = (K * T) // P + E
    ROW = D + 4
    SP_PAIRS = NJ // 2
    PAIRS = SP_PAIRS + TILES // 2
    RING = 4
    U = B * C
    SCALE = 1.0 / float(D) ** 0.5
    NO_TOKEN = 1.0e6
    assert (TILES % 2, NJ % 2, (PAIRS - SP_PAIRS) % RING, SP_PAIRS % RING) == (0, 0, 0, 0)

    slots = nc.dram_tensor("slots", (TILES * P, ROW), F32).ap()
    routed = nc.dram_tensor("routed", (K * T, D), F32).ap()

    with ExitStack() as ctx:
        def sb(name, shape, dt=F32):
            return ctx.enter_context(nc.sbuf_tensor(name, shape, dt))

        def sem(name):
            return ctx.enter_context(nc.semaphore(name))

        bank = [ctx.enter_context(nc.psum_tensor(f"bank{i}", [P, 512], F32)) for i in range(8)]

        x_tok = sb("x_tok", [P, NJ, D])
        rows = sb("rows", [P, NJ, ROW])
        h_feat = sb("h_feat", [P, C, T])
        q_feat = sb("q_feat", [P, C, T])
        e_feat = sb("e_feat", [P, C, T])
        s_feat = sb("s_feat", [P, C, T])
        p_feat = sb("p_feat", [P, C, T])
        m_feat = sb("m_feat", [P, C, T])
        w_attn = sb("w_attn", [P, 5, C, D])
        col = sb("col", [P, NCOL * C + C * E + E])
        bias_s = sb("bias_s", [P, 2, C])
        w_stage = sb("w_stage", [P, 2, EW])
        w_hi = sb("w_hi", [P, NX, EW], F32R)
        w_lo = sb("w_lo", [P, NX, EW], F32R)
        r_hi = sb("r_hi", [P, C, E], F32R)
        r_lo = sb("r_lo", [P, C, E], F32R)
        xh = sb("xh", [P, RING, 2, C, P], F32R)
        xl = sb("xl", [P, RING, 2, C, P], F32R)
        ah = sb("ah", [P, 2, 2, P], F32R)
        al = sb("al", [P, 2, 2, P], F32R)
        x_tiles = s_feat[:].rearrange("p c (r d) -> p (c r) d", d=2 * D).rearrange("p r (t d) -> p r t d", t=2)
        y_tiles = p_feat[:].rearrange("p c (r d) -> p (c r) d", d=2 * D).rearrange("p r (t d) -> p r t d", t=2)
        y_shared = q_feat[:].rearrange("p c (j d) -> p (c j) d", d=D)
        y_choice = [h_feat[:].rearrange("p c (j d) -> p (c j) d", d=D),
                    m_feat[:].rearrange("p c (j d) -> p (c j) d", d=D)]
        act_t = w_attn[:, 0].rearrange("p c (t i) -> p c t i", t=2)
        silu_t = w_attn[:, 1].rearrange("p c (t i) -> p c t i", t=2)
        pad_row = sb("pad_row", [P, ROW])
        ident = sb("ident", [P, P])
        earlier = sb("earlier", [P, P], BF16)
        ones_bf = sb("ones_bf", [P, P], BF16)
        idx_i = sb("idx_i", [P, E + TILES + NJ], I32)
        idx_f = sb("idx_f", [P, E + TILES + NJ])
        rev_e, tile_no, tok_no = idx_f[:, 0:E], idx_f[:, E:E + TILES], idx_f[:, E + TILES:]
        stats = sb("stats", [P, NJ, 6])
        mv = sb("mv", [P, 4, NJ, 2])
        ln_t = sb("ln_t", [P, 4, 7, NJ])
        router = p_feat[:].rearrange("p c t -> p (c t)")
        rt = router[:, 0:12 * NJ * E].rearrange("p (n j e) -> p n j e", j=NJ, e=E)
        cmp = router[:, 12 * NJ * E:].rearrange("p (m e) -> p m e", e=E)
        chosen = sb("chosen", [P, NJ, E], BF16)
        rs = w_attn[:, 2, 1, 0:12 * NJ].rearrange("p (n j) -> p n j", j=NJ)
        ex = w_attn[:, 2, 1, 12 * NJ:12 * NJ + 4 * E].rearrange("p (n e) -> p n e", e=E)
        ex_i = sb("ex_i", [P, 2, E], I32)
        tile_e = w_attn[:, 2, 0, 0:4 * TILES].rearrange("p (n m) -> p n m", m=TILES)
        tile_e_i = sb("tile_e_i", [1, TILES], I32)
        slot_of = sb("slot_of", [P, K, NJ], U32)
        meta = w_attn[:, 2, 0, 4 * TILES:8 * TILES].rearrange("p (m n) -> p m n", n=4)
        slot_w = sb("slot_w", [P, TILES])
        slot_row = sb("slot_row", [P, TILES], U32)

        g_col, b_col, bq, bqa, bk, bka, bv = [col[:, i * C:(i + 1) * C] for i in range(NCOL)]
        wr = col[:, NCOL * C:NCOL * C + C * E].rearrange("p (c e) -> p c e", c=C)
        r_bias = col[:, NCOL * C + C * E:]
        WQ, WQA, WK, WKA, WV = range(5)

        x_in = [sem(f"x_in{b}") for b in range(B)]
        col_in, wqk_in, wrest_in = sem("col_in"), sem("wqk_in"), sem("wrest_in")
        stage_in = [sem("stage_in0"), sem("stage_in1")]
        pad_made, pad_out = sem("pad_made"), sem("pad_out")
        consts, consts2 = sem("consts"), sem("consts2")
        v_chain = sem("v_chain")
        var_ready, root_ln, root_ready, norm_ready = (sem(n) for n in ("var_ready", "root_ln", "root_ready", "norm_ready"))
        shift_ready, shifted = sem("shift_ready"), sem("shifted")
        hat_ready = sem("hat_ready")
        hT_psum, hT_ready = sem("hT_psum"), sem("hT_ready")
        q_psum, q_ready = sem("q_psum"), sem("q_ready")
        qa_psum, e_ready, sum_ready, log_ready, inv_ready = (sem(n) for n in ("qa_psum", "e_ready", "sum_ready", "log_ready", "inv_ready"))
        eq_ready, k_psum, mix_ready, v_psum, a_ready = (sem(n) for n in ("eq_ready", "k_psum", "mix_ready", "v_psum", "a_ready"))
        ka_psum = sem("ka_psum")
        w_hi_ready, w_lo_ready, r_split = sem("w_hi_ready"), sem("w_lo_ready"), sem("r_split")
        bias_ready = sem("bias_ready")
        aT_psum, x1_ready, xn_ready = sem("aT_psum"), sem("x1_ready"), sem("xn_ready")
        logits_psum, logits_ready, exp_ready = sem("logits_psum"), sem("logits_ready"), sem("exp_ready")
        chosen_ready, rank_psum, slot_ready, tile_e_ready = (sem(n) for n in ("chosen_ready", "rank_psum", "slot_ready", "tile_e_ready"))
        rows_out, meta_in, slot_meta = sem("rows_out"), sem("meta_in"), sem("slot_meta")
        xt_in = [sem(f"xt_in{u}") for u in range(RING)]
        t_done, hi_done, lo_done, gu_done, silu_done, act_done = (sem(n) for n in ("t_done", "hi_done", "lo_done", "gu_done", "silu_done", "act_done"))
        a_done, ah_done, al_done, d_done = (sem(n) for n in ("a_done", "ah_done", "al_done", "d_done"))
        y_done = [sem("y_done_even"), sem("y_done_odd")]
        y_out = [sem(f"y_out{u}") for u in range(RING)]
        yc_in = [sem(f"yc_in{i}") for i in range(4)]
        o_ready, o_out = sem("o_ready"), sem("o_out")

        def tok_tiles(dram, j0, n):
            return dram.rearrange("(j p) d -> p j d", p=P)[:, j0:j0 + n, :]

        x_rows = x.rearrange("b s d -> (b s) d")
        out_rows = out.rearrange("b s d -> (b s) d")
        ATT_BANKS = [(0, 1), (2, 3), (4, 5), (6, 7)]

        def routed_steps(engine, before, body, after):
            for p in before:
                body(p)
            loops, rest = divmod(after[0] - before[-1] - 1, RING)
            assert rest == 0
            with engine.Fori(0, loops, 1) as i:
                for u in range(RING):
                    body(before[-1] + 1 + u, i * RING)
            for p in after:
                body(p)

        FIRST = SP_PAIRS
        STEPS_BEFORE = range(FIRST - 1, FIRST + 6)
        STEPS_AFTER = range(PAIRS - 2, PAIRS + 2)

        N_IN, N_ATT, N_FFN, N_OUT = range(4)
        norm_order = [(N_IN, 0), (N_IN, 1), (N_ATT, 0), (N_FFN, 0), (N_ATT, 1), (N_FFN, 1), (N_OUT, 0), (N_OUT, 1)]

        block = ctx.enter_context(nc.Block())

        @block.sync
        def _(sp):
            for b in range(B):
                sp.dma_start(x_tok[:, b * JB:(b + 1) * JB], tok_tiles(x_rows, b * JB, JB)).then_inc(x_in[b], 16)
                if b == 0:
                    sp.dma_start(col[:], misc).then_inc(col_in, 16)
            sp.dma_start(w_attn[:, 0:3], attn_w[:, 0:3]).then_inc(wqk_in, 16)
            sp.dma_start(w_attn[:, 3:5], attn_w[:, 3:5]).then_inc(wrest_in, 16)
            for e in range(NX):
                if e >= 2:
                    sp.wait_ge(w_lo_ready, e - 1)
                sp.dma_start(w_stage[:, e % 2], expert_w[:, e]).then_inc(stage_in[e % 2], 16)
                if e == 3:
                    sp.wait_ge(pad_made, 2)
                    sp.dma_start(slots.rearrange("(m p) d -> p m d", p=P),
                                 pad_row[:].rearrange("p (o d) -> p o d", o=1).to_broadcast([P, TILES, ROW])
                                 ).then_inc(pad_out, 16)
            sp.wait_ge(rows_out, 16 * K * NJ)
            sp.dma_start(meta[:], slots.rearrange("(m p) d -> p m d", p=P)[:, :, D:ROW]).then_inc(meta_in, 16)

            def load(p, i=0):
                u = p % RING
                if not (isinstance(i, int) and p < FIRST + RING):
                    sp.wait_ge(t_done, i + p - RING + 1)
                sp.dma_start(x_tiles[:, u],
                             slots.rearrange("(m t p) d -> m p t d", p=P, t=2)[bass.ds(i + p - FIRST, 1), :, :, 0:D]
                             .rearrange("o p t d -> (o p) t d")).then_inc(xt_in[u], 16)

            sp.wait_ge(inv_ready, 2 * U)
            for p in range(FIRST, FIRST + RING):
                load(p)
            with sp.Fori(0, (PAIRS - FIRST) // RING - 1, 1) as i:
                for u in range(RING):
                    load(FIRST + RING + u, i * RING)
            for u in range(RING):
                sp.wait_ge(y_out[u], 32 * (PAIRS - FIRST) // RING)
            for b in range(B):
                for k in range(K):
                    sp.dma_start(y_choice[k][:, b * JB:(b + 1) * JB], tok_tiles(routed, k * NJ + b * JB, JB)
                                 ).then_inc(yc_in[2 * b + k], 16)
            for b in range(B):
                sp.wait_ge(o_ready, (b + 1) * JB)
                sp.dma_start(tok_tiles(out_rows, b * JB, JB), e_feat[:].rearrange("p c (j d) -> p (c j) d", d=D)[:, b * JB:(b + 1) * JB]).then_inc(o_out, 16)
            sp.wait_ge(o_out, 16 * B)

        @block.tensor
        def _(pe):
            def att_bank(pair, c):
                return bank[ATT_BANKS[pair][c]]

            def transposed(pair, b):
                pe.wait_ge(hat_ready, (b + 1) * JB)
                for c in range(C):
                    for j in range(JB):
                        last = pe.transpose(att_bank(pair, c)[:, j * P:(j + 1) * P],
                                            rows[:, b * JB + j, c * P:(c + 1) * P], ident[:])
                    last.then_inc(hT_psum, 1)

            def project(w, src, pair, b, done):
                for oc in range(C):
                    for ic in range(C):
                        last = pe.matmul(att_bank(pair, oc)[:], w_attn[:, w, ic, oc * P:(oc + 1) * P],
                                         src[:, ic, b * S:(b + 1) * S], start=ic == 0, stop=ic == C - 1)
                    last.then_inc(done, 1)

            pe.wait_ge(consts2, 2)
            transposed(0, 0)
            transposed(1, 1)
            pe.wait_ge(wqk_in, 16)
            pe.wait_ge(hT_ready, C)
            project(WQ, h_feat, 2, 0, q_psum)
            pe.wait_ge(hT_ready, 2 * C)
            project(WQ, h_feat, 3, 1, q_psum)
            pe.wait_ge(q_ready, C)
            project(WQA, q_feat, 0, 0, qa_psum)
            project(WK, h_feat, 1, 0, k_psum)
            pe.wait_ge(q_ready, 2 * C)
            project(WQA, q_feat, 2, 1, qa_psum)
            project(WK, h_feat, 3, 1, k_psum)
            pe.wait_ge(wrest_in, 16)
            pe.wait_ge(mix_ready, C)
            pe.wait_ge(e_ready, U)
            project(WKA, m_feat, 0, 0, ka_psum)
            project(WV, h_feat, 2, 0, v_psum)
            pe.wait_ge(mix_ready, 2 * C)
            project(WKA, m_feat, 1, 1, ka_psum)
            project(WV, h_feat, 3, 1, v_psum)
            for b, pair in ((0, 0), (1, 2)):
                pe.wait_ge(a_ready, (b + 1) * C)
                pe.wait_ge(e_ready, U + (b + 1) * C)
                for j in range(JB):
                    for c in range(C):
                        last = pe.transpose(bank[ATT_BANKS[pair][j // 2]][:, (j % 2) * D + c * P:(j % 2) * D + (c + 1) * P],
                                            e_feat[:, c, b * S + j * P:b * S + (j + 1) * P], ident[:])
                    if j % 2:
                        last.then_inc(aT_psum, 1)

            def turn(p, i=0):
                u, par = p % RING, p % 2
                if p < SP_PAIRS:
                    pe.wait_ge(xn_ready, 2 * p + 2)
                else:
                    pe.wait_ge(xt_in[u], 16 * ((p - FIRST) // RING + 1) + (i * (16 // RING)))
                if p >= 2:
                    pe.wait_ge(lo_done, i + p - 1)
                for t in range(2):
                    for c in range(C):
                        src = rows[:, 2 * p + t, c * P:(c + 1) * P] if p < SP_PAIRS else x_tiles[:, u, t, c * P:(c + 1) * P]
                        last = pe.transpose(bank[2 + par][:, (t * C + c) * P:(t * C + c + 1) * P], src, ident[:])
                last.then_inc(t_done, 1)

            def gate_up(p, i=0):
                u, par = p % RING, p % 2
                experts = tile_experts(p)
                pe.wait_ge(lo_done, i + p + 1)
                if p >= 2:
                    pe.wait_ge(act_done, i + p - 1)
                for t in range(2):
                    dst = bank[4 + par][:, t * GU:(t + 1) * GU]
                    parts = [(a, w, c) for c in range(C) for a, w in ((xh, w_hi), (xh, w_lo))] + [(xl, w_hi, c) for c in range(C)]
                    for n, (a, w, c) in enumerate(parts):
                        last = pe.matmul(dst, a[:, u, t, c, :], w[:, bass.ds(experts[t], 1), c * GU:(c + 1) * GU],
                                         start=n == 0, stop=n == len(parts) - 1)
                last.then_inc(gu_done, 1)

            def turn_act(p, i=0):
                par = p % 2
                pe.wait_ge(act_done, i + p + 1)
                if p >= 2:
                    pe.wait_ge(al_done, i + p - 1)
                for t in range(2):
                    last = pe.transpose(bank[6 + par][:, t * P:(t + 1) * P], act_t[:, par, t, :], ident[:])
                last.then_inc(a_done, 1)

            def down(p, i=0):
                par = p % 2
                experts = tile_experts(p)
                pe.wait_ge(al_done, i + p + 1)
                if p >= 2:
                    pe.wait_ge(y_done[par], i // 2 + p // 2)
                for t in range(2):
                    dst = bank[par][:, t * D:(t + 1) * D]
                    parts = ((ah, w_hi), (ah, w_lo), (al, w_hi))
                    for n, (a, w) in enumerate(parts):
                        last = pe.matmul(dst, a[:, par, t, :], w[:, bass.ds(experts[t], 1), C * GU:C * GU + D],
                                         start=n == 0, stop=n == len(parts) - 1)
                last.then_inc(d_done, 1)

            expert_reg = [[pe.alloc_register(f"expert_{u}_{t}") for t in range(2)] for u in range(RING)]

            def load_experts(p, i=0):
                pe.load(expert_reg[p % RING], tile_e_i[0:1, bass.ds((i + (p - FIRST)) * 2, 2)])

            def tile_experts(p):
                if p < SP_PAIRS:
                    return E, E
                return [nc.s_assert_within(pe.snap(r), 0, E - 1, skip_runtime_bounds_check_because="a minimum with E - 1 wrote it")
                        for r in expert_reg[p % RING]]

            def logits(p):
                pe.wait_ge(lo_done, p + 1)
                for t in range(2):
                    dst = bank[0][:, (2 * p + t) * E:(2 * p + t + 1) * E]
                    parts = [(a, w, c) for c in range(C) for a, w in ((xh, r_hi), (xh, r_lo), (xl, r_hi))]
                    for n, (a, w, c) in enumerate(parts):
                        last = pe.matmul(dst, a[:, p, t, c, :], w[:, c, :], start=n == 0, stop=n == len(parts) - 1)
                last.then_inc(logits_psum, 1)

            pe.wait_ge(r_split, 2)
            pe.wait_ge(x1_ready, JB)
            for b in range(B):
                for p in (2 * b, 2 * b + 1):
                    turn(p)
                for p in (2 * b, 2 * b + 1):
                    logits(p)
            pe.wait_ge(x1_ready, 2 * JB)
            pe.wait_ge(w_lo_ready, NX)
            gate_up(0)
            gate_up(1)
            pe.wait_ge(chosen_ready, 1)
            flat = chosen[:].rearrange("p j e -> p (j e)")
            pe.matmul(bank[1][:, 0:NJ * E], earlier[:], flat, start=True, stop=False, skip_group_check=True)
            for j in range(1, NJ):
                last = pe.matmul(bank[1][:, j * E:NJ * E], ones_bf[:], flat[:, 0:(NJ - j) * E], start=False, stop=j == NJ - 1,
                                 skip_group_check=True)
            last.then_inc(rank_psum, 1)
            for j in range(NJ):
                last = pe.matmul(bank[7][:, 256:256 + E], ones_bf[:], chosen[:, j, :], start=j == 0, stop=j == NJ - 1)
            last.then_inc(rank_psum, 1)
            turn_act(0)
            gate_up(2)
            pe.wait_ge(slot_ready, 1)
            pe.wait_ge(logits_ready, 1)
            turn_act(1)
            down(0)
            gate_up(3)
            turn_act(2)
            down(1)
            turn_act(3)
            down(2)
            down(3)
            pe.wait_ge(tile_e_ready, 1)
            load_experts(FIRST)
            turn(FIRST)

            def step(p, i=0):
                if FIRST <= p < PAIRS:
                    gate_up(p, i)
                if FIRST <= p + 1 < PAIRS and p >= FIRST:
                    load_experts(p + 1, i)
                if p + 2 < PAIRS or not isinstance(i, int):
                    turn(p + 2, i)
                if FIRST <= p - 1 < PAIRS:
                    turn_act(p - 1, i)
                if FIRST <= p - 2 < PAIRS:
                    down(p - 2, i)

            routed_steps(pe, STEPS_BEFORE, step, STEPS_AFTER)

        @block.scalar
        def _(act):
            act.preload_act_table_set("natural_log_exp_and_others")

            def roots(n, lo, hi):
                act.wait_ge(var_ready, n)
                i, b = norm_order[n - 1]
                act.activation(ln_t[:, i, 1, lo:hi], ln_t[:, i, 0, lo:hi], ACT.Ln).then_inc(root_ln, 1)
                act.wait_ge(root_ln, n)
                act.activation(ln_t[:, i, 2, lo:hi], ln_t[:, i, 1, lo:hi], ACT.Exp, scale=-0.5).then_inc(root_ready, 1)

            def shift(n, b):
                act.wait_ge(shift_ready, n)
                i = (N_ATT, N_OUT)[(n - 1) // B]
                for j in range(b * JB, (b + 1) * JB):
                    act.activation(x_tok[:, j], x_tok[:, j], ACT.Identity, bias=ln_t[:, i, 6, j:j + 1]).then_inc(shifted, 1)

            def split_hi(n):
                for e in range(split_hi.next, min(split_hi.next + n, NX)):
                    act.wait_ge(stage_in[e % 2], 16 * (e // 2 + 1))
                    act.activation(w_hi[:, e], w_stage[:, e % 2], ACT.Copy).then_inc(w_hi_ready, 1)
                split_hi.next = min(split_hi.next + n, NX)
            split_hi.next = 0

            def affine(b):
                for c in range(C):
                    act.wait_ge(hT_psum, b * C + c + 1)
                    act.activation(h_feat[:, c, b * S:(b + 1) * S], bank[ATT_BANKS[b][c]][:], ACT.Identity,
                                   bias=b_col[:, c:c + 1], scale=g_col[:, c:c + 1]).then_inc(hT_ready, 1)

            def query(b):
                for c in range(C):
                    act.wait_ge(q_psum, b * C + c + 1)
                    act.activation(q_feat[:, c, b * S:(b + 1) * S], bank[ATT_BANKS[2 + b][c]][:], ACT.Identity,
                                   bias=bq[:, c:c + 1]).then_inc(q_ready, 1)

            def exps(which, b, pair, psum_ready):
                for c in range(C):
                    act.wait_ge(psum_ready, b * C + c + 1)
                    if which:
                        act.wait_ge(eq_ready, b * C + c + 1)
                    act.activation(e_feat[:, c, b * S:(b + 1) * S], bank[ATT_BANKS[pair][c]][:], ACT.Exp,
                                   bias=bias_s[:, which, c:c + 1], scale=SCALE).then_inc(e_ready, 1)

            def inverse(which, b):
                for c in range(C):
                    n = which * U + b * C + c
                    unit = s_feat[:, c, b * S:(b + 1) * S]
                    act.wait_ge(sum_ready, n + 1)
                    act.activation(unit, unit, ACT.Ln).then_inc(log_ready, 1)
                for c in range(C):
                    n = which * U + b * C + c
                    unit = s_feat[:, c, b * S:(b + 1) * S]
                    act.wait_ge(log_ready, n + 1)
                    act.activation(unit, unit, ACT.Exp, scale=-1.0).then_inc(inv_ready, 1)

            def hi(p, i=0):
                u, par = p % RING, p % 2
                act.wait_ge(t_done, i + p + 1)
                if p >= RING:
                    act.wait_ge(gu_done, i + p - RING + 1)
                act.activation(xh[:, u].rearrange("p t c s -> p (t c s)"), bank[2 + par][:], ACT.Copy).then_inc(hi_done, 1)

            def silu(p, i=0):
                par = p % 2
                act.wait_ge(gu_done, i + p + 1)
                if p >= 2:
                    act.wait_ge(act_done, i + p - 1)
                act.activation(silu_t[:, par], bank[4 + par][:].rearrange("p (t g) -> p t g", t=2)[:, :, 0:P],
                               ACT.Silu).then_inc(silu_done, 1)

            def act_hi(p, i=0):
                par = p % 2
                act.wait_ge(a_done, i + p + 1)
                if p >= 2:
                    act.wait_ge(d_done, i + p - 1)
                act.activation(ah[:, par].rearrange("p t s -> p (t s)"), bank[6 + par][:, 0:2 * P], ACT.Copy).then_inc(ah_done, 1)

            def y_odd(p, i=0):
                if p % 2 == 0:
                    return
                u = p % RING
                act.wait_ge(d_done, i + p + 1)
                if p < SP_PAIRS:
                    act.activation(y_shared[:, 2 * p:2 * p + 2].rearrange("p t d -> p (t d)"), bank[1][:], ACT.Copy).then_inc(y_done[1], 1)
                    return
                if p >= FIRST + RING:
                    act.wait_ge(y_out[u], 32 * ((p - FIRST) // RING) + i * (32 // RING))
                if p == FIRST + 1:
                    act.wait_ge(slot_meta, 2)
                for t in range(2):
                    last = act.activation(y_tiles[:, u, t], bank[1][:, t * D:(t + 1) * D], ACT.Copy,
                                          scale=slot_w[:, bass.ds((i + p - FIRST) * 2 + t, 1)])
                last.then_inc(y_done[1], 1)

            act.wait_ge(col_in, 16)
            roots(1, 0, JB)
            roots(2, JB, NJ)
            affine(0)
            affine(1)
            split_hi(1)
            query(0)
            act.wait_ge(bias_ready, 2)
            query(1)
            split_hi(1)
            exps(0, 0, 0, qa_psum)
            inverse(0, 0)
            split_hi(1)
            exps(0, 1, 2, qa_psum)
            inverse(0, 1)
            split_hi(3)
            exps(1, 0, 0, ka_psum)
            split_hi(1)
            inverse(1, 0)
            split_hi(2)
            exps(1, 1, 1, ka_psum)
            split_hi(1)
            inverse(1, 1)
            split_hi(1)
            roots(3, 0, JB)
            shift(1, 0)
            split_hi(1)
            roots(4, 0, JB)
            split_hi(1)
            roots(5, JB, NJ)
            hi(0)
            hi(1)
            shift(2, 1)
            roots(6, JB, NJ)
            split_hi(1)
            hi(2)
            hi(3)
            act.wait_ge(logits_ready, 1)
            act.activation(rt[:, 2], rt[:, 1], ACT.Exp).then_inc(exp_ready, 1)
            split_hi(NX)
            silu(0)
            silu(1)
            act_hi(0)
            silu(2)
            act_hi(1)
            silu(3)
            act_hi(2)
            y_odd(1)
            act_hi(3)
            y_odd(3)
            hi(FIRST)

            def step(p, i=0):
                if p + 2 < PAIRS or not isinstance(i, int):
                    hi(p + 2, i)
                if FIRST <= p < PAIRS:
                    silu(p, i)
                if FIRST <= p - 1 < PAIRS:
                    act_hi(p - 1, i)
                if FIRST <= p - 2 < PAIRS:
                    y_odd(p - 2, i)

            routed_steps(act, STEPS_BEFORE, step, STEPS_AFTER)
            act.preload_act_table_set("natural_log_exp_and_others")
            roots(7, 0, JB)
            shift(3, 0)
            roots(8, JB, NJ)
            shift(4, 1)

        @block.vector
        def _(v):
            steps = [0]

            def chain(ins):
                steps[0] += 1
                ins.then_inc(v_chain, 1)
                v.wait_ge(v_chain, steps[0])

            def statistics(n, srcs, scale, eps):
                i, b = norm_order[n - 1]
                lo, hi_ = b * JB, (b + 1) * JB
                for j, src in zip(range(lo, hi_), srcs):
                    last = v.bn_stats(stats[:, j, :], src)
                chain(last)
                for j in range(lo, hi_):
                    last = v.bn_aggr(mv[:, i, j, :], stats[:, j, :])
                chain(last)
                v.tensor_scalar(ln_t[:, i, 0, lo:hi_], mv[:, i, lo:hi_, 1], scale, eps, ALU.mult, ALU.add).then_inc(var_ready, 1)

            def refine(n, want_shift=False):
                i, b = norm_order[n - 1]
                a = slice(b * JB, (b + 1) * JB)
                v.wait_ge(root_ready, n)
                chain(v.tensor_tensor(ln_t[:, i, 3, a], ln_t[:, i, 2, a], ln_t[:, i, 2, a], ALU.mult))
                chain(v.scalar_tensor_tensor(ln_t[:, i, 4, a], ln_t[:, i, 3, a], -0.5, ln_t[:, i, 0, a], ALU.mult, ALU.mult))
                chain(v.scalar_tensor_tensor(ln_t[:, i, 5, a], ln_t[:, i, 4, a], 1.5, ln_t[:, i, 2, a], ALU.add, ALU.mult))
                if want_shift:
                    v.scalar_tensor_tensor(ln_t[:, i, 6, a], mv[:, i, a, 0], -1.0, ln_t[:, i, 5, a], ALU.mult, ALU.mult).then_inc(shift_ready, 1)

            def normalise(n, src, dst, ready):
                i, b = norm_order[n - 1]
                for j in range(b * JB, (b + 1) * JB):
                    v.tensor_scalar(dst[:, j, 0:D], src[:, j], mv[:, i, j, 0:1], ln_t[:, i, 5, j:j + 1],
                                    ALU.subtract, ALU.mult).then_inc(ready, 1)

            v.wait_ge(consts, 1)
            for b in range(B):
                v.wait_ge(x_in[b], 16)
                statistics(b + 1, [x_tok[:, j] for j in range(b * JB, (b + 1) * JB)], 1.0 + LN_EPS, LN_EPS * LN_EPS)
            for b in range(B):
                refine(b + 1)
                normalise(b + 1, x_tok, rows, hat_ready)
                if b == 0:
                    v.wait_ge(col_in, 16)
                    v.tensor_scalar(bias_s[:, 0], bqa, SCALE, None, ALU.mult).then_inc(bias_ready, 1)
                    v.tensor_scalar(bias_s[:, 1], bka, SCALE, None, ALU.mult).then_inc(bias_ready, 1)
                    v.tensor_copy(r_hi[:], wr).then_inc(r_split, 1)
                    v.wait_ge(r_split, 1)
                    v.tensor_tensor(r_lo[:], wr, r_hi[:].bitcast(F32), ALU.subtract).then_inc(r_split, 1)

            def cumulate(which, b):
                for c in range(C):
                    n = which * U + b * C + c
                    a = slice(b * S, (b + 1) * S)
                    v.wait_ge(e_ready, n + 1)
                    v.tensor_tensor_scan(s_feat[:, c, a], e_feat[:, c, a], e_feat[:, c, a], 0.0, ALU.add, ALU.bypass).then_inc(sum_ready, 1)

            def pool_query(b, pair):
                a = slice(b * S, (b + 1) * S)
                for c in range(C):
                    n = b * C + c
                    v.wait_ge(inv_ready, n + 1)
                    v.wait_ge(eq_ready, n + 1)
                    chain(v.tensor_tensor(s_feat[:, c, a], q_feat[:, c, a], s_feat[:, c, a], ALU.mult))
                    chain(v.tensor_tensor_scan(p_feat[:, c, a], s_feat[:, c, a], s_feat[:, c, a], 0.0, ALU.add, ALU.bypass))
                    v.wait_ge(k_psum, n + 1)
                    v.scalar_tensor_tensor(m_feat[:, c, a], bank[ATT_BANKS[pair][c]][:], bk[:, c:c + 1], p_feat[:, c, a],
                                           ALU.add, ALU.mult).then_inc(mix_ready, 1)

            def pool_keys(b, pair):
                a = slice(b * S, (b + 1) * S)
                for c in range(C):
                    n = b * C + c
                    v.wait_ge(inv_ready, U + n + 1)
                    v.wait_ge(eq_ready, U + n + 1)
                    chain(v.tensor_tensor(s_feat[:, c, a], m_feat[:, c, a], s_feat[:, c, a], ALU.mult))
                    chain(v.tensor_tensor_scan(p_feat[:, c, a], s_feat[:, c, a], s_feat[:, c, a], 0.0, ALU.add, ALU.bypass))
                    v.wait_ge(v_psum, n + 1)
                    v.scalar_tensor_tensor(e_feat[:, c, a], bank[ATT_BANKS[pair][c]][:], bv[:, c:c + 1], p_feat[:, c, a],
                                           ALU.add, ALU.mult).then_inc(a_ready, 1)

            def att_rows(b, j):
                return bank[ATT_BANKS[2 * b][j // 2]][:, (j % 2) * D:(j % 2 + 1) * D]

            def att_statistics(b):
                v.wait_ge(aT_psum, 2 * b + 2)
                statistics((3, 5)[b], [att_rows(b, j) for j in range(JB)], 1.0, LN_EPS)

            def residual(b):
                refine((3, 5)[b], True)
                for j in range(JB):
                    jj = b * JB + j
                    v.wait_ge(shifted, jj + 1)
                    last = v.scalar_tensor_tensor(x_tok[:, jj], att_rows(b, j), ln_t[:, N_ATT, 5, jj:jj + 1], x_tok[:, jj],
                                                  ALU.mult, ALU.add)
                    last.then_inc(x1_ready, 1)
                v.wait_ge(x1_ready, (b + 1) * JB)
                statistics((4, 6)[b], [x_tok[:, b * JB + j] for j in range(JB)], 1.0, LN_EPS)

            def lo(p, i=0):
                u, par = p % RING, p % 2
                v.wait_ge(hi_done, i + p + 1)
                v.tensor_tensor(xl[:, u].rearrange("p t c s -> p (t c s)"), bank[2 + par][:],
                                xh[:, u].rearrange("p t c s -> p (t c s)").bitcast(F32), ALU.subtract).then_inc(lo_done, 1)

            def gated(p, i=0):
                par = p % 2
                v.wait_ge(silu_done, i + p + 1)
                if p >= 2:
                    v.wait_ge(a_done, i + p - 1)
                v.tensor_tensor(act_t[:, par], silu_t[:, par], bank[4 + par][:].rearrange("p (t g) -> p t g", t=2)[:, :, P:GU],
                                ALU.mult).then_inc(act_done, 1)

            def act_lo(p, i=0):
                par = p % 2
                v.wait_ge(ah_done, i + p + 1)
                v.tensor_tensor(al[:, par].rearrange("p t s -> p (t s)"), bank[6 + par][:, 0:2 * P],
                                ah[:, par].rearrange("p t s -> p (t s)").bitcast(F32), ALU.subtract).then_inc(al_done, 1)

            def y_even(p, i=0):
                if p % 2:
                    return
                u = p % RING
                v.wait_ge(d_done, i + p + 1)
                if p < SP_PAIRS:
                    v.tensor_copy(y_shared[:, 2 * p:2 * p + 2].rearrange("p t d -> p (t d)"), bank[0][:]).then_inc(y_done[0], 1)
                    return
                if p >= FIRST + RING:
                    v.wait_ge(y_out[u], 32 * ((p - FIRST) // RING) + i * (32 // RING))
                for t in range(2):
                    last = v.tensor_scalar(y_tiles[:, u, t], bank[0][:, t * D:(t + 1) * D],
                                           slot_w[:, bass.ds((i + p - FIRST) * 2 + t, 1)], None, ALU.mult)
                last.then_inc(y_done[0], 1)

            cumulate(0, 0)
            pool_query(0, 1)
            cumulate(0, 1)
            pool_query(1, 3)
            cumulate(1, 0)
            pool_keys(0, 2)
            cumulate(1, 1)
            att_statistics(0)
            pool_keys(1, 3)
            residual(0)
            refine(4)
            normalise(4, x_tok, rows, xn_ready)
            att_statistics(1)
            lo(0)
            lo(1)
            residual(1)
            refine(6)
            normalise(6, x_tok, rows, xn_ready)
            lo(2)
            lo(3)

            def over_e(a):
                return a.rearrange("p (j o) -> p j o", o=1).to_broadcast([P, NJ, E])

            def over_j(a):
                return a.rearrange("p (o e) -> p o e", o=1).to_broadcast([P, NJ, E])

            v.wait_ge(logits_psum, SP_PAIRS)
            chain(v.tensor_tensor(rt[:, 0], bank[0][:, 0:NJ * E].rearrange("p (j e) -> p j e", e=E), over_j(r_bias), ALU.add))
            chain(v.tensor_reduce(rs[:, 0], rt[:, 0], AX_X, ALU.max))
            v.tensor_tensor(rt[:, 1], rt[:, 0], over_e(rs[:, 0]), ALU.subtract).then_inc(logits_ready, 1)
            v.wait_ge(exp_ready, 1)
            prob = rt[:, 2]
            best = []
            for k in range(K):
                chain(v.tensor_reduce(rs[:, 1 + 2 * k], prob, AX_X, ALU.max))
                chain(v.tensor_tensor(rt[:, 3 + 3 * k], prob, over_e(rs[:, 1 + 2 * k]), ALU.is_equal))
                chain(v.tensor_tensor(rt[:, 4 + 3 * k], rt[:, 3 + 3 * k], over_j(rev_e), ALU.mult))
                chain(v.tensor_reduce(rs[:, 2 + 2 * k], rt[:, 4 + 3 * k], AX_X, ALU.max))
                chain(v.tensor_tensor(rt[:, 5 + 3 * k], rt[:, 4 + 3 * k], over_e(rs[:, 2 + 2 * k]), ALU.is_equal))
                best.append(rt[:, 5 + 3 * k])
                if k == 0:
                    chain(v.scalar_tensor_tensor(rt[:, 9], best[0], -4.0, prob, ALU.mult, ALU.add))
                    prob = rt[:, 9]
            v.tensor_tensor(chosen[:], best[0], best[1], ALU.add).then_inc(chosen_ready, 1)
            chain(v.tensor_reduce(rs[:, 5], rt[:, 2], AX_X, ALU.add))
            chain(v.scalar_tensor_tensor(rs[:, 6], rs[:, 5], TOPK_EPS, rs[:, 1], ALU.mult, ALU.add))
            chain(v.tensor_tensor(rs[:, 7], rs[:, 6], rs[:, 3], ALU.add))
            chain(v.reciprocal(rs[:, 8], rs[:, 7]))
            v.tensor_copy(rows[:, :, D], rs[:, 2])
            v.tensor_tensor(rows[:, :, D + 1], rs[:, 1], rs[:, 8], ALU.mult)
            v.tensor_tensor(rows[:, :, D + 2], rs[:, 3], rs[:, 8], ALU.mult)
            v.tensor_copy(rows[:, :, D + 3], tok_no)
            v.wait_ge(rank_psum, 2)
            chain(v.tensor_scalar(ex_i[:, 0], bank[7][:, 256:256 + E], float(P - 1), None, ALU.add))
            chain(v.tensor_scalar(ex_i[:, 1], ex_i[:, 0], P.bit_length() - 1, None, ALU.logical_shift_right))
            chain(v.tensor_copy(ex[:, 0], ex_i[:, 1]))
            chain(v.tensor_tensor_scan(ex[:, 1], ex[:, 0], ex[:, 0], 0.0, ALU.add, ALU.bypass))
            chain(v.tensor_tensor(ex[:, 2], ex[:, 1], ex[:, 0], ALU.subtract))
            chain(v.tensor_scalar(ex[:, 3], ex[:, 2], float(P), None, ALU.mult))
            chain(v.tensor_tensor(rt[:, 10], bank[1][:, 0:NJ * E].rearrange("p (j e) -> p j e", e=E), over_j(ex[:, 3]), ALU.add))
            for k in range(K):
                chain(v.tensor_tensor(rt[:, 11] if k else rt[:, 0], rt[:, 10], best[k], ALU.mult))
                last = v.tensor_reduce(rs[:, 9 + k], rt[:, 11] if k else rt[:, 0], AX_X, ALU.add)
                chain(last)
            v.tensor_copy(slot_of[:], rs[:, 9:9 + K]).then_inc(slot_ready, 1)
            chain(v.tensor_tensor(cmp[:], ex[:, 1].rearrange("p (o e) -> p o e", o=1).to_broadcast([P, TILES, E]),
                                  tile_no.rearrange("p (m o) -> p m o", o=1).to_broadcast([P, TILES, E]), ALU.is_le))
            chain(v.tensor_reduce(tile_e[:, 0], cmp[:], AX_X, ALU.add))
            chain(v.tensor_scalar(tile_e[:, 1], tile_e[:, 0], float(E - 1), None, ALU.min))
            v.tensor_copy(tile_e_i[:], tile_e[0:1, 1]).then_inc(tile_e_ready, 1)
            chain(v.tensor_scalar(tile_e[:, 2], tile_e[:, 1], -1.0, float(E), ALU.mult, ALU.add))
            gated(0)
            gated(1)
            act_lo(0)
            gated(2)
            act_lo(1)
            y_even(0)
            gated(3)
            act_lo(2)
            act_lo(3)
            y_even(2)
            v.wait_ge(meta_in, 16)
            chain(v.tensor_tensor(tile_e[:, 3], meta[:, :, 0], tile_e[:, 2], ALU.is_equal))
            chain(v.tensor_tensor(cmp[:, :, 0], meta[:, :, 1], meta[:, :, 2], ALU.subtract))
            chain(v.tensor_tensor(cmp[:, :, 1], cmp[:, :, 0], tile_e[:, 3], ALU.mult))
            v.tensor_tensor(slot_w[:], cmp[:, :, 1], meta[:, :, 2], ALU.add).then_inc(slot_meta, 1)
            chain(v.tensor_scalar(cmp[:, :, 2], tile_e[:, 3], -float(T), float(T), ALU.mult, ALU.add))
            v.tensor_tensor(slot_row[:], cmp[:, :, 2], meta[:, :, 3], ALU.add).then_inc(slot_meta, 1)
            v.wait_ge(slot_meta, 2)
            lo(FIRST)

            def step(p, i=0):
                if p + 2 < PAIRS or not isinstance(i, int):
                    lo(p + 2, i)
                if FIRST <= p < PAIRS:
                    gated(p, i)
                if FIRST <= p - 1 < PAIRS:
                    act_lo(p - 1, i)
                if FIRST <= p - 2 < PAIRS:
                    y_even(p - 2, i)

            routed_steps(v, STEPS_BEFORE, step, STEPS_AFTER)

            total = s_feat[:].rearrange("p c (j d) -> p (c j) d", d=D)
            result = e_feat[:].rearrange("p c (j d) -> p (c j) d", d=D)
            v.wait_ge(y_done[1], PAIRS // 2)
            for b in range(B):
                for k in range(K):
                    v.wait_ge(yc_in[2 * b + k], 16)
                a = slice(b * JB, (b + 1) * JB)
                chain(v.tensor_tensor(total[:, a], y_choice[0][:, a], y_choice[1][:, a], ALU.add))
                chain(v.tensor_tensor(total[:, a], total[:, a], y_shared[:, a], ALU.add))
                statistics(7 + b, [total[:, j] for j in range(b * JB, (b + 1) * JB)], 1.0, LN_EPS)
            for b in range(B):
                refine(7 + b, True)
                for j in range(b * JB, (b + 1) * JB):
                    v.wait_ge(shifted, NJ + j + 1)
                    v.scalar_tensor_tensor(result[:, j], total[:, j], ln_t[:, N_OUT, 5, j:j + 1], x_tok[:, j],
                                           ALU.mult, ALU.add).then_inc(o_ready, 1)

        @block.gpsimd
        def _(g):
            g.memset(ident[:], 0.0).then_inc(consts, 1)
            g.memset(pad_row[:], 0.0).then_inc(pad_made, 1)
            g.memset(earlier[:], 1.0).then_inc(consts, 1)
            g.memset(ones_bf[:], 1.0).then_inc(consts, 1)
            g.wait_ge(consts, 3)
            g.affine_select(out=ident[:], in_=ident[:], compare_op=ALU.not_equal, fill=1.0, base=0,
                            pattern=[[-1, P]], channel_multiplier=1).then_inc(consts2, 1)
            g.affine_select(out=earlier[:], in_=earlier[:], compare_op=ALU.is_gt, fill=0.0, base=0,
                            pattern=[[1, P]], channel_multiplier=-1).then_inc(consts2, 1)
            g.wait_ge(pad_made, 1)
            g.memset(pad_row[:, D + 3:D + 4], NO_TOKEN).then_inc(pad_made, 1)
            g.iota(idx_i[:, 0:E], [[-1, E]], base=E, channel_multiplier=0).then_inc(consts, 1)
            g.iota(idx_i[:, E:E + TILES], [[1, TILES]], base=0, channel_multiplier=0).then_inc(consts, 1)
            g.iota(idx_i[:, E + TILES:], [[P, NJ]], base=0, channel_multiplier=1).then_inc(consts, 1)
            g.wait_ge(consts, 6)
            g.tensor_copy(idx_f[:], idx_i[:]).then_inc(consts2, 1)

            def split_lo(n):
                for e in range(split_lo.next, min(split_lo.next + n, NX)):
                    g.wait_ge(w_hi_ready, e + 1)
                    g.tensor_tensor(w_lo[:, e], w_stage[:, e % 2], w_hi[:, e].bitcast(F32), ALU.subtract).then_inc(w_lo_ready, 1)
                split_lo.next = min(split_lo.next + n, NX)
            split_lo.next = 0

            def weighted(which, b):
                src = m_feat if which else q_feat
                for c in range(C):
                    a = slice(b * S, (b + 1) * S)
                    g.wait_ge(e_ready, which * U + b * C + c + 1)
                    if not which:
                        g.wait_ge(qa_psum, (b + 1) * C)
                    else:
                        g.wait_ge(ka_psum, (b + 1) * C)
                    g.tensor_tensor(src[:, c, a], e_feat[:, c, a], src[:, c, a], ALU.mult).then_inc(eq_ready, 1)

            split_lo(1)
            split_lo(1)
            weighted(0, 0)
            split_lo(1)
            weighted(0, 1)
            split_lo(3)
            weighted(1, 0)
            split_lo(3)
            weighted(1, 1)
            split_lo(NX)
            g.wait_ge(pad_out, 16)
            g.wait_ge(slot_ready, 1)
            for j in range(NJ):
                for k in range(K):
                    g.indirect_dma_start(out=slots, out_offset=bass.IndirectOffsetOnAxis(slot_of[:, k, j:j + 1], 0),
                                         in_=rows[:, j, :], in_offset=None).then_inc(rows_out, 16)

            g.wait_ge(slot_meta, 2)
            for p in range(FIRST, PAIRS):
                g.wait_ge(y_done[p % 2], p // 2 + 1)
                for t in range(2):
                    m = (p - FIRST) * 2 + t
                    g.indirect_dma_start(out=routed, out_offset=bass.IndirectOffsetOnAxis(slot_row[:, m:m + 1], 0),
                                         in_=y_tiles[:, p % RING, t], in_offset=None, bounds_check=K * T - 1,
                                         oob_is_err=False).then_inc(y_out[p % RING], 16)


def kernel(**inputs):
    import numpy as np
    import concourse.bacc as bacc
    from concourse.bass_utils import run_bass_kernel_spmd

    a = {n: np.asarray(v) for n, v in inputs.items()}
    x = np.ascontiguousarray(a["L0_attn_hidden_states"])
    D = x.shape[2]
    C = D // P
    attn_w = np.stack([a["L0_attn_" + n].T.reshape(C, P, D) for n in ("Wq", "Wqa", "Wk", "Wka", "Wv")])
    attn_w = np.ascontiguousarray(attn_w.transpose(2, 0, 1, 3))
    cols = np.stack([a["L0_attn_" + n].reshape(C, P) for n in ("ln_g", "ln_b", "bq", "bqa", "bk", "bka", "bv")])
    wr = a["L0_ffn_Wr"].T.reshape(C, P, -1)
    E = wr.shape[2]
    misc = np.concatenate([cols.transpose(2, 0, 1).reshape(P, -1), wr.transpose(1, 0, 2).reshape(P, -1),
                           np.broadcast_to(a["L0_ffn_bias"], (P, E))], axis=1)
    misc = np.ascontiguousarray(misc)
    wg = np.concatenate([a["L0_ffn_Wg"], a["L0_ffn_sWg"][None]])
    wu = np.concatenate([a["L0_ffn_Wu"], a["L0_ffn_sWu"][None]])
    wd = np.concatenate([a["L0_ffn_Wd"], a["L0_ffn_sWd"][None]])
    gu = np.concatenate([wg, wu], axis=2).reshape(E + 1, C, P, -1).transpose(2, 0, 1, 3).reshape(P, E + 1, -1)
    expert_w = np.ascontiguousarray(np.concatenate([gu, wd.transpose(1, 0, 2)], axis=2))

    nc = bacc.Bacc("TRN2", target_bir_lowering=False, num_devices=1)
    arrays = {"x": x, "attn_w": attn_w, "misc": misc, "expert_w": expert_w}
    args = [nc.dram_tensor(n, v.shape, mybir.dt.from_np(v.dtype), kind="ExternalInput").ap() for n, v in arrays.items()]
    out = nc.dram_tensor("out", x.shape, F32, kind="ExternalOutput").ap()
    block_kernel(nc, *args, out)
    r = run_bass_kernel_spmd(nc, [arrays], core_ids=[0])
    return r.results[0]["out"]
```

```python
from contextlib import ExitStack

import concourse.bass as bass
from concourse import mybir

F32 = mybir.dt.float32
F32R = mybir.dt.float32r
BF16 = mybir.dt.bfloat16
I32 = mybir.dt.int32
U32 = mybir.dt.uint32
ALU = mybir.AluOpType
ACT = mybir.ActivationFunctionType
AX_X = mybir.AxisListType.X

P = 128
LN_EPS = 1e-5
TOPK_EPS = 1e-9


def block_kernel(nc, x, attn_w, misc, expert_w, out):
    B, S, D = x.shape
    T = B * S
    C = D // P
    NJ = T // P
    JB = S // P
    _, NX, EW = expert_w.shape
    E = NX - 1
    GU = 2 * P
    NCOL = 7
    K = 2
    TILES = (K * T) // P + E
    ROW = D + 1
    SP_PAIRS = NJ // 2
    PAIRS = SP_PAIRS + TILES // 2
    RING = 4
    U = B * C
    SCALE = 1.0 / float(D) ** 0.5
    WARM_START, WARM_FIRST, WARM_ROUTER, WARM_UP = 20, 5, 7, 9
    OUT_GROUPS = 4
    OG = NJ // OUT_GROUPS
    ROUND = 1.5 * 2.0 ** 23
    NO_ROW = 1 << 20
    assert (TILES % 2, NJ % 2, (PAIRS - SP_PAIRS) % RING, SP_PAIRS % RING) == (0, 0, 0, 0)

    slots = nc.dram_tensor("slots", (TILES * P, ROW), F32).ap()
    routed = nc.dram_tensor("routed", (K * T, D), F32).ap()

    with ExitStack() as ctx:
        def sb(name, shape, dt=F32):
            return ctx.enter_context(nc.sbuf_tensor(name, shape, dt))

        def sem(name):
            return ctx.enter_context(nc.semaphore(name))

        bank = [ctx.enter_context(nc.psum_tensor(f"bank{i}", [P, 512], F32)) for i in range(8)]

        x_tok = sb("x_tok", [P, NJ, D])
        rows = sb("rows", [P, NJ, ROW])
        h_feat = sb("h_feat", [P, C, T])
        q_feat = sb("q_feat", [P, C, T])
        e_feat = sb("e_feat", [P, C, T])
        s_mem = sb("s_mem", [P, RING * 2 * ROW])
        s_feat = s_mem[:, 0:C * T].rearrange("p (c t) -> p c t", c=C)
        p_feat = sb("p_feat", [P, C, T])
        m_feat = sb("m_feat", [P, C, T])
        w_attn = sb("w_attn", [P, 5, C, D])
        col = sb("col", [P, NCOL * C + C * E + 1])
        bias_s = sb("bias_s", [P, 2, C])
        w_stage = sb("w_stage", [P, 2, EW])
        row_halves = rows[:].rearrange("p (b j) d -> p b (j d)", b=B)
        stages = [w_stage[:, 0], w_stage[:, 1], row_halves[:, 0, 0:EW], row_halves[:, 1, 0:EW]]
        w_hi = sb("w_hi", [P, NX, EW], F32R)
        w_lo = sb("w_lo", [P, NX, EW], F32R)
        r_hi = sb("r_hi", [P, C, E], F32R)
        r_lo = sb("r_lo", [P, C, E], F32R)
        xh = sb("xh", [P, RING, 2, C, P], F32R)
        xl = sb("xl", [P, RING, 2, C, P], F32R)
        ah = sb("ah", [P, 2, 2, P], F32R)
        al = sb("al", [P, 2, 2, P], F32R)
        x_tiles = s_mem[:].rearrange("p (r t d) -> p r t d", r=RING, t=2)
        y_tiles = p_feat[:].rearrange("p c (r d) -> p (c r) d", d=2 * D).rearrange("p r (t d) -> p r t d", t=2)
        y_shared = q_feat[:].rearrange("p c (j d) -> p (c j) d", d=D)
        y_choice = [h_feat[:].rearrange("p c (j d) -> p (c j) d", d=D),
                    m_feat[:].rearrange("p c (j d) -> p (c j) d", d=D)]
        act_t = w_attn[:, 0].rearrange("p c (t i) -> p c t i", t=2)
        silu_t = w_attn[:, 1].rearrange("p c (t i) -> p c t i", t=2)
        total = s_feat.rearrange("p c (j d) -> p (c j) d", d=D)
        result = e_feat[:].rearrange("p c (j d) -> p (c j) d", d=D)
        logits_t = m_feat[0:E, 0]
        pad_row = sb("pad_row", [P, ROW])
        ident = sb("ident", [P, P])
        earlier = sb("earlier", [P, P], BF16)
        ones_bf = sb("ones_bf", [P, P], BF16)
        idx_i = sb("idx_i", [P, E + TILES], I32)
        idx_f = sb("idx_f", [P, E + TILES])
        rev_e, tile_no = idx_f[:, 0:E], idx_f[:, E:]
        row_no = sb("row_no", [P, K, NJ], I32)
        stats = sb("stats", [P, NJ, 6])
        mv = sb("mv", [P, 4, NJ, 2])
        ln_t = sb("ln_t", [P, 4, 7, NJ])
        router = p_feat[:].rearrange("p c t -> p (c t)")
        rt = router[:, 0:12 * NJ * E].rearrange("p (n j e) -> p n j e", j=NJ, e=E)
        cmp = router[:, 12 * NJ * E:].rearrange("p (m e) -> p m e", e=E)
        chosen = sb("chosen", [P, NJ, E], BF16)
        warm_rows = ones_bf[:].rearrange("p (o i) -> p o i", o=1).to_broadcast([P, 4, P])
        rs = w_attn[:, 2, 1, 0:10 * NJ].rearrange("p (n j) -> p n j", j=NJ)
        ex = w_attn[:, 2, 1, 10 * NJ:10 * NJ + 4 * E].rearrange("p (n e) -> p n e", e=E)
        before = w_attn[:, 2, 0, 4 * TILES:4 * TILES + E + 1]
        tile_e = w_attn[:, 2, 0, 0:4 * TILES].rearrange("p (n m) -> p n m", m=TILES)
        tile_e_i = sb("tile_e_i", [1, TILES], I32)
        slot_of = sb("slot_of", [P, K, NJ], U32)
        gate_w = sb("gate_w", [P, K, NJ])
        slot_row = sb("slot_row", [P, TILES], U32)

        g_col, b_col, bq, bqa, bk, bka, bv = [col[:, i * C:(i + 1) * C] for i in range(NCOL)]
        wr = col[:, NCOL * C:NCOL * C + C * E].rearrange("p (c e) -> p c e", c=C)
        r_bias = col[0:E, NCOL * C + C * E:]
        WQ, WQA, WK, WKA, WV = range(5)

        x_in = [sem(f"x_in{b}") for b in range(B)]
        col_in, wq_in, wqk_in, wrest_in = sem("col_in"), sem("wq_in"), sem("wqk_in"), sem("wrest_in")
        stage_in = [sem(f"stage_in{i}") for i in range(4)]
        pad_made, pad_out = sem("pad_made"), sem("pad_out")
        consts, consts2, row_nos = sem("consts"), sem("consts2"), sem("row_nos")
        v_chain = sem("v_chain")
        var_ready, root_ln, root_ready = (sem(n) for n in ("var_ready", "root_ln", "root_ready"))
        shift_ready, out_normed = sem("shift_ready"), sem("out_normed")
        hat_ready = sem("hat_ready")
        hT_psum, hT_ready = sem("hT_psum"), sem("hT_ready")
        q_psum, q_ready = sem("q_psum"), sem("q_ready")
        qa_psum, e_ready, sum_ready, log_ready, inv_ready = (sem(n) for n in ("qa_psum", "e_ready", "sum_ready", "log_ready", "inv_ready"))
        eq_ready, k_psum, mix_ready, v_psum, a_ready = (sem(n) for n in ("eq_ready", "k_psum", "mix_ready", "v_psum", "a_ready"))
        ka_psum = sem("ka_psum")
        w_hi_act = sem("w_hi_act")
        r_split, logits_t_psum, logits_t_ready = sem("r_split"), sem("logits_t_psum"), sem("logits_t_ready")
        w_lo_pool, w_lo_dve = sem("w_lo_pool"), sem("w_lo_dve")
        bias_ready = sem("bias_ready")
        aT_psum, att_ready, x1_ready, xn_ready = sem("aT_psum"), sem("att_ready"), sem("x1_ready"), sem("xn_ready")
        logits_psum, logits_ready, exp_ready = sem("logits_psum"), sem("logits_ready"), sem("exp_ready")
        chosen_ready, rank_psum, slot_ready, tile_e_ready = (sem(n) for n in ("chosen_ready", "rank_psum", "slot_ready", "tile_e_ready"))
        rows_out = [[sem(f"rows_out{k}{b}") for b in range(B)] for k in range(K)]
        id_ready, row_nos_kept, gates_ready = sem("id_ready"), sem("row_nos_kept"), sem("gates_ready")
        xt_in = [sem(f"xt_in{u}") for u in range(RING)]
        t_done, hi_done, lo_done, gu_done, silu_done, act_done = (sem(n) for n in ("t_done", "hi_done", "lo_done", "gu_done", "silu_done", "act_done"))
        a_done, ah_done, al_done, d_done = (sem(n) for n in ("a_done", "ah_done", "al_done", "d_done"))
        y_done = [sem("y_done_even"), sem("y_done_odd")]
        y_out = [sem(f"y_out{u}") for u in range(RING)]
        yc_in = [sem(f"yc_in{o}") for o in range(OUT_GROUPS)]
        first_weighted, first_and_shared = sem("first_weighted"), sem("first_and_shared")
        o_ready, o_out = [sem(f"o_ready{o}") for o in range(OUT_GROUPS)], sem("o_out")

        plan = [(0, "dve"), (1, "dve"), (2, "dve"), (0, "dve"), (1, "pool"), (2, "pool"), (3, "pool"), (0, "pool"),
                (1, "dve"), (2, "dve"), (3, "pool"), (0, "pool"), (1, "dve"), (2, "pool"), (3, "pool"), (0, "pool"), (1, "pool")]
        N_DVE = sum(who == "dve" for _, who in plan)

        def expert_at(n):
            return (n - 1) % NX

        def fills(n):
            return sum(plan[m][0] == plan[n][0] for m in range(n + 1))

        def taken_by(who):
            return [n for n in range(NX) if plan[n][1] == who]

        def wait_stage_free(engine, n):
            last = [m for m in range(n) if plan[m][0] == plan[n][0]]
            if last:
                who = plan[last[-1]][1]
                engine.wait_ge(w_lo_dve if who == "dve" else w_lo_pool, taken_by(who).index(last[-1]) + 1)

        def tok_tiles(dram, j0, n):
            return dram.rearrange("(j p) d -> p j d", p=P)[:, j0:j0 + n, :]

        x_rows = x.rearrange("b s d -> (b s) d")
        out_rows = out.rearrange("b s d -> (b s) d")
        ATT_BANKS = [(0, 1), (2, 3), (4, 5), (6, 7)]

        def routed_steps(engine, before, body, after):
            for p in before:
                body(p)
            loops, rest = divmod(after[0] - before[-1] - 1, RING)
            assert rest == 0
            with engine.Fori(0, loops, 1) as i:
                for u in range(RING):
                    body(before[-1] + 1 + u, i * RING)
            for p in after:
                body(p)

        FIRST = SP_PAIRS
        STEPS_BEFORE = range(FIRST - 1, FIRST + 6)
        STEPS_AFTER = range(PAIRS - 2, PAIRS + 2)

        N_IN, N_ATT, N_FFN, N_OUT = range(4)
        norm_order = [(i, slice(b * JB, (b + 1) * JB)) for i, b in
                      ((N_IN, 0), (N_IN, 1), (N_ATT, 0), (N_ATT, 1), (N_FFN, 0), (N_FFN, 1))]
        norm_order += [(N_OUT, slice(o * OG, (o + 1) * OG)) for o in range(OUT_GROUPS)]

        def add_x1(engine, groups):
            for o in groups:
                for j in range(o * OG, (o + 1) * OG):
                    engine.wait_ge(out_normed, j + 1)
                    engine.tensor_tensor(result[:, j], total[:, j], x_tok[:, j], ALU.add).then_inc(o_ready[o], 1)

        block = ctx.enter_context(nc.Block())

        @block.sync
        def _(sp):
            sp.dma_start(x_tok[:, 0:JB], tok_tiles(x_rows, 0, JB)).then_inc(x_in[0], 16)
            sp.dma_start(col[:], misc).then_inc(col_in, 16)
            sp.dma_start(w_attn[:, 0:1], attn_w[:, 0:1]).then_inc(wq_in, 16)
            for b in range(1, B):
                sp.dma_start(x_tok[:, b * JB:(b + 1) * JB], tok_tiles(x_rows, b * JB, JB)).then_inc(x_in[b], 16)
            sp.dma_start(w_attn[:, 1:3], attn_w[:, 1:3]).then_inc(wqk_in, 16)
            for n in range(NX):
                stage = plan[n][0]
                if stage >= 2 and fills(n) == 1:
                    sp.wait_ge(hT_psum, (stage - 1) * C)
                wait_stage_free(sp, n)
                sp.dma_start(stages[stage], expert_w[:, expert_at(n)]).then_inc(stage_in[stage], 16)
                if n == 3:
                    sp.dma_start(w_attn[:, 3:5], attn_w[:, 3:5]).then_inc(wrest_in, 16)
            sp.wait_ge(pad_made, 2)
            sp.dma_start(slots.rearrange("(m p) d -> p m d", p=P),
                         pad_row[:].rearrange("p (o d) -> p o d", o=1).to_broadcast([P, TILES, ROW])
                         ).then_inc(pad_out, 16)
            for k in range(K):
                for b in range(B):
                    sp.wait_ge(rows_out[k][b], 16 * JB)

            def load(p, i=0):
                u = p % RING
                if not (isinstance(i, int) and p < FIRST + RING):
                    sp.wait_ge(row_nos_kept, i + p - RING - FIRST + 1)
                sp.dma_start(x_tiles[:, u],
                             slots.rearrange("(m t p) d -> m p t d", p=P, t=2)[bass.ds(i + p - FIRST, 1)]
                             .rearrange("o p t d -> (o p) t d")).then_inc(xt_in[u], 16)

            sp.wait_ge(inv_ready, 2 * U)
            for p in range(FIRST, FIRST + RING):
                load(p)
            with sp.Fori(0, (PAIRS - FIRST) // RING - 1, 1) as i:
                for u in range(RING):
                    load(FIRST + RING + u, i * RING)
            for u in range(RING):
                sp.wait_ge(y_out[u], 32 * (PAIRS - FIRST) // RING)
            for o in range(OUT_GROUPS):
                for k in range(K):
                    sp.dma_start(y_choice[k][:, o * OG:(o + 1) * OG], tok_tiles(routed, k * NJ + o * OG, OG)).then_inc(yc_in[o], 16)
            for o in range(OUT_GROUPS):
                sp.wait_ge(o_ready[o], OG)
                sp.dma_start(tok_tiles(out_rows, o * OG, OG), result[:, o * OG:(o + 1) * OG]).then_inc(o_out, 16)
            sp.wait_ge(o_out, 16 * OUT_GROUPS)

        @block.tensor
        def _(pe):
            def att_bank(pair, c):
                return bank[ATT_BANKS[pair][c]]

            def transposed(pair, b):
                pe.wait_ge(hat_ready, (b + 1) * JB)
                for c in range(C):
                    for j in range(JB):
                        last = pe.transpose(att_bank(pair, c)[:, j * P:(j + 1) * P],
                                            rows[:, b * JB + j, c * P:(c + 1) * P], ident[:])
                    last.then_inc(hT_psum, 1)

            def project(w, src, pair, b, done):
                for oc in range(C):
                    for ic in range(C):
                        last = pe.matmul(att_bank(pair, oc)[:], w_attn[:, w, ic, oc * P:(oc + 1) * P],
                                         src[:, ic, b * S:(b + 1) * S], start=ic == 0, stop=ic == C - 1)
                    last.then_inc(done, 1)

            def keep_warm(n):
                for _ in range(n):
                    pe.matmul(bank[7][:], ones_bf[:], warm_rows, start=True, stop=True)

            pe.wait_ge(consts2, 2)
            keep_warm(WARM_START)
            transposed(0, 0)
            keep_warm(WARM_FIRST)
            pe.wait_ge(wq_in, 16)
            pe.wait_ge(hT_ready, C)
            project(WQ, h_feat, 2, 0, q_psum)
            transposed(1, 1)
            pe.wait_ge(wqk_in, 16)
            pe.wait_ge(q_ready, C)
            project(WQA, q_feat, 0, 0, qa_psum)
            pe.wait_ge(hT_ready, 2 * C)
            project(WK, h_feat, 1, 0, k_psum)
            project(WQ, h_feat, 3, 1, q_psum)
            pe.wait_ge(q_ready, 2 * C)
            project(WQA, q_feat, 2, 1, qa_psum)
            project(WK, h_feat, 3, 1, k_psum)
            pe.wait_ge(wrest_in, 16)
            pe.wait_ge(mix_ready, C)
            pe.wait_ge(e_ready, C)
            project(WKA, m_feat, 0, 0, ka_psum)
            pe.wait_ge(mix_ready, 2 * C)
            project(WKA, m_feat, 1, 1, ka_psum)
            pe.wait_ge(e_ready, U)
            project(WV, h_feat, 2, 0, v_psum)

            def att_transposed(b, pair):
                pe.wait_ge(a_ready, (b + 1) * C)
                pe.wait_ge(e_ready, U + (b + 1) * C)
                for j in range(JB):
                    for c in range(C):
                        last = pe.transpose(bank[ATT_BANKS[pair][j // 2]][:, (j % 2) * D + c * P:(j % 2) * D + (c + 1) * P],
                                            e_feat[:, c, b * S + j * P:b * S + (j + 1) * P], ident[:])
                    if j % 2:
                        last.then_inc(aT_psum, 1)

            project(WV, h_feat, 3, 1, v_psum)
            att_transposed(0, 0)
            att_transposed(1, 2)

            def turn(p, i=0):
                u, par = p % RING, p % 2
                if p < SP_PAIRS:
                    pe.wait_ge(xn_ready, 2 * p + 2)
                else:
                    pe.wait_ge(xt_in[u], 16 * ((p - FIRST) // RING + 1) + (i * (16 // RING)))
                if p >= 2:
                    pe.wait_ge(lo_done, i + p - 1)
                for t in range(2):
                    for c in range(C):
                        src = rows[:, 2 * p + t, c * P:(c + 1) * P] if p < SP_PAIRS else x_tiles[:, u, t, c * P:(c + 1) * P]
                        last = pe.transpose(bank[2 + par][:, (t * C + c) * P:(t * C + c + 1) * P], src, ident[:])
                last.then_inc(t_done, 1)

            def gate_up(p, i=0):
                u, par = p % RING, p % 2
                experts = tile_experts(p)
                pe.wait_ge(lo_done, i + p + 1)
                if p >= 2:
                    pe.wait_ge(act_done, i + p - 1)
                for t in range(2):
                    dst = bank[4 + par][:, t * GU:(t + 1) * GU]
                    parts = [(a, w, c) for c in range(C) for a, w in ((xh, w_hi), (xh, w_lo))] + [(xl, w_hi, c) for c in range(C)]
                    for n, (a, w, c) in enumerate(parts):
                        last = pe.matmul(dst, a[:, u, t, c, :], w[:, bass.ds(experts[t], 1), c * GU:(c + 1) * GU],
                                         start=n == 0, stop=n == len(parts) - 1)
                last.then_inc(gu_done, 1)

            def turn_act(p, i=0):
                par = p % 2
                pe.wait_ge(act_done, i + p + 1)
                if p >= 2:
                    pe.wait_ge(al_done, i + p - 1)
                for t in range(2):
                    last = pe.transpose(bank[6 + par][:, t * P:(t + 1) * P], act_t[:, par, t, :], ident[:])
                last.then_inc(a_done, 1)

            def down(p, i=0):
                par = p % 2
                experts = tile_experts(p)
                pe.wait_ge(al_done, i + p + 1)
                if p >= 2:
                    pe.wait_ge(y_done[par], i // 2 + p // 2)
                for t in range(2):
                    dst = bank[par][:, t * D:(t + 1) * D]
                    parts = ((ah, w_hi), (ah, w_lo), (al, w_hi))
                    for n, (a, w) in enumerate(parts):
                        last = pe.matmul(dst, a[:, par, t, :], w[:, bass.ds(experts[t], 1), C * GU:C * GU + D],
                                         start=n == 0, stop=n == len(parts) - 1)
                last.then_inc(d_done, 1)

            expert_reg = [[pe.alloc_register(f"expert_{u}_{t}") for t in range(2)] for u in range(RING)]

            def load_experts(p, i=0):
                pe.load(expert_reg[p % RING], tile_e_i[0:1, bass.ds((i + (p - FIRST)) * 2, 2)])

            def tile_experts(p):
                if p < SP_PAIRS:
                    return E, E
                return [nc.s_assert_within(pe.snap(r), 0, E - 1, skip_runtime_bounds_check_because="a minimum with E - 1 wrote it")
                        for r in expert_reg[p % RING]]

            def logits(b):
                pe.wait_ge(lo_done, 2 * b + 2)
                parts = [(a, w, c) for c in range(C) for a, w in ((xh, r_hi), (xh, r_lo), (xl, r_hi))]
                for n, (a, w, c) in enumerate(parts):
                    last = pe.matmul(bank[6 + b][0:E, :], w[:, c, :], a[:, 2 * b:2 * b + 2, :, c, :].rearrange("e p t s -> e (p t) s"),
                                     start=n == 0, stop=n == len(parts) - 1)
                last.then_inc(logits_t_psum, 1)

            def logits_by_token(b):
                pe.wait_ge(logits_t_ready, b + 1)
                for j in range(b * JB, (b + 1) * JB):
                    last = pe.transpose(bank[0][:, j * E:(j + 1) * E], logits_t[:, j * P:(j + 1) * P], ident[0:E, 0:E])
                last.then_inc(logits_psum, 1)

            pe.wait_ge(r_split, 2)
            pe.wait_ge(x1_ready, JB)
            keep_warm(WARM_UP)
            turn(0)
            turn(1)
            keep_warm(WARM_ROUTER)
            turn(2)
            logits(0)
            turn(3)
            logits_by_token(0)
            logits(1)
            logits_by_token(1)
            pe.wait_ge(x1_ready, 2 * JB)
            pe.wait_ge(w_lo_dve, 1)
            gate_up(0)
            gate_up(1)
            pe.wait_ge(chosen_ready, 1)
            flat = chosen[:].rearrange("p j e -> p (j e)")
            pe.matmul(bank[1][:, 0:NJ * E], earlier[:], flat, start=True, stop=False, skip_group_check=True)
            for j in range(1, NJ):
                last = pe.matmul(bank[1][:, j * E:NJ * E], ones_bf[:], flat[:, 0:(NJ - j) * E], start=False, stop=j == NJ - 1,
                                 skip_group_check=True)
            last.then_inc(rank_psum, 1)
            for j in range(NJ):
                last = pe.matmul(bank[7][:, 256:256 + E], ones_bf[:], chosen[:, j, :], start=j == 0, stop=j == NJ - 1)
            last.then_inc(rank_psum, 1)
            turn_act(0)
            gate_up(2)
            pe.wait_ge(slot_ready, 1)
            turn_act(1)
            down(0)
            gate_up(3)
            turn_act(2)
            down(1)
            turn_act(3)
            down(2)
            down(3)
            pe.wait_ge(tile_e_ready, 1)
            load_experts(FIRST)
            pe.wait_ge(al_done, SP_PAIRS)
            pe.wait_ge(rows_out[K - 1][B - 1], 16 * JB)
            keep_warm(WARM_UP)
            pe.wait_ge(w_lo_dve, N_DVE)
            pe.wait_ge(w_lo_pool, NX - N_DVE)
            turn(FIRST)

            def step(p, i=0):
                if FIRST <= p < PAIRS:
                    gate_up(p, i)
                if FIRST <= p + 1 < PAIRS and p >= FIRST:
                    load_experts(p + 1, i)
                if p + 2 < PAIRS or not isinstance(i, int):
                    turn(p + 2, i)
                if FIRST <= p - 1 < PAIRS:
                    turn_act(p - 1, i)
                if FIRST <= p - 2 < PAIRS:
                    down(p - 2, i)

            routed_steps(pe, STEPS_BEFORE, step, STEPS_AFTER)

        @block.scalar
        def _(act):
            act.preload_act_table_set("natural_log_exp_and_others")

            def roots(n):
                act.wait_ge(var_ready, n)
                i, a = norm_order[n - 1]
                act.activation(ln_t[:, i, 1, a], ln_t[:, i, 0, a], ACT.Ln).then_inc(root_ln, 1)
                act.wait_ge(root_ln, n)
                act.activation(ln_t[:, i, 2, a], ln_t[:, i, 1, a], ACT.Exp, scale=-0.5).then_inc(root_ready, 1)

            def attention_norm(n, b):
                i, a = norm_order[n - 1]
                act.wait_ge(shift_ready, n - 2)
                for j in range(a.start, a.stop):
                    rows_psum = bank[ATT_BANKS[2 * b][(j % JB) // 2]][:, (j % 2) * D:(j % 2 + 1) * D]
                    act.activation(rows[:, j, 0:D], rows_psum, ACT.Identity, bias=ln_t[:, i, 6, j:j + 1],
                                   scale=ln_t[:, i, 5, j:j + 1]).then_inc(att_ready, 1)

            def normalise(n):
                i, a = norm_order[n - 1]
                act.wait_ge(shift_ready, n - 2)
                for j in range(a.start, a.stop):
                    act.activation(rows[:, j, 0:D], x_tok[:, j], ACT.Identity, bias=ln_t[:, i, 6, j:j + 1],
                                   scale=ln_t[:, i, 5, j:j + 1]).then_inc(xn_ready, 1)

            def logits_bias(b):
                act.wait_ge(logits_t_psum, b + 1)
                act.activation(logits_t[:, b * S:(b + 1) * S], bank[6 + b][0:E, :], ACT.Identity, bias=r_bias
                               ).then_inc(logits_t_ready, 1)

            pool_experts = taken_by("pool")

            def split_hi(first, last):
                for n in pool_experts[first:last]:
                    act.wait_ge(stage_in[plan[n][0]], 16 * fills(n))
                    act.activation(w_hi[:, expert_at(n)], stages[plan[n][0]], ACT.Copy).then_inc(w_hi_act, 1)

            def affine(b):
                for c in range(C):
                    act.wait_ge(hT_psum, b * C + c + 1)
                    act.activation(h_feat[:, c, b * S:(b + 1) * S], bank[ATT_BANKS[b][c]][:], ACT.Identity,
                                   bias=b_col[:, c:c + 1], scale=g_col[:, c:c + 1]).then_inc(hT_ready, 1)

            def query(b):
                for c in range(C):
                    act.wait_ge(q_psum, b * C + c + 1)
                    act.activation(q_feat[:, c, b * S:(b + 1) * S], bank[ATT_BANKS[2 + b][c]][:], ACT.Identity,
                                   bias=bq[:, c:c + 1]).then_inc(q_ready, 1)

            def exps(which, b, pair, psum_ready):
                for c in range(C):
                    act.wait_ge(psum_ready, b * C + c + 1)
                    if which:
                        act.wait_ge(eq_ready, b * C + c + 1)
                    act.activation(e_feat[:, c, b * S:(b + 1) * S], bank[ATT_BANKS[pair][c]][:], ACT.Exp,
                                   bias=bias_s[:, which, c:c + 1], scale=SCALE).then_inc(e_ready, 1)

            def inverse(which, b):
                for c in range(C):
                    n = which * U + b * C + c
                    unit = s_feat[:, c, b * S:(b + 1) * S]
                    act.wait_ge(sum_ready, n + 1)
                    act.activation(unit, unit, ACT.Ln).then_inc(log_ready, 1)
                for c in range(C):
                    n = which * U + b * C + c
                    unit = s_feat[:, c, b * S:(b + 1) * S]
                    act.wait_ge(log_ready, n + 1)
                    act.activation(unit, unit, ACT.Exp, scale=-1.0).then_inc(inv_ready, 1)

            def hi(p, i=0):
                u, par = p % RING, p % 2
                act.wait_ge(t_done, i + p + 1)
                if p >= RING:
                    act.wait_ge(gu_done, i + p - RING + 1)
                act.activation(xh[:, u].rearrange("p t c s -> p (t c s)"), bank[2 + par][:], ACT.Copy).then_inc(hi_done, 1)

            def silu(p, i=0):
                par = p % 2
                act.wait_ge(gu_done, i + p + 1)
                if p >= 2:
                    act.wait_ge(act_done, i + p - 1)
                act.activation(silu_t[:, par], bank[4 + par][:].rearrange("p (t g) -> p t g", t=2)[:, :, 0:P],
                               ACT.Silu).then_inc(silu_done, 1)

            def act_hi(p, i=0):
                par = p % 2
                act.wait_ge(a_done, i + p + 1)
                if p >= 2:
                    act.wait_ge(d_done, i + p - 1)
                act.activation(ah[:, par].rearrange("p t s -> p (t s)"), bank[6 + par][:, 0:2 * P], ACT.Copy).then_inc(ah_done, 1)

            def y_odd(p, i=0):
                if p % 2 == 0:
                    return
                u = p % RING
                act.wait_ge(d_done, i + p + 1)
                if p < SP_PAIRS:
                    act.activation(y_shared[:, 2 * p:2 * p + 2].rearrange("p t d -> p (t d)"), bank[1][:], ACT.Copy).then_inc(y_done[1], 1)
                    return
                if p >= FIRST + RING:
                    act.wait_ge(y_out[u], 32 * ((p - FIRST) // RING) + i * (32 // RING))
                act.activation(y_tiles[:, u].rearrange("p t d -> p (t d)"), bank[1][:], ACT.Copy).then_inc(y_done[1], 1)

            act.wait_ge(col_in, 16)
            roots(1)
            affine(0)
            roots(2)
            query(0)
            affine(1)
            split_hi(0, 1)
            act.wait_ge(bias_ready, 2)
            exps(0, 0, 0, qa_psum)
            inverse(0, 0)
            query(1)
            split_hi(1, 4)
            exps(0, 1, 2, qa_psum)
            inverse(0, 1)
            split_hi(4, 5)
            exps(1, 0, 0, ka_psum)
            inverse(1, 0)
            exps(1, 1, 1, ka_psum)
            split_hi(5, 6)
            inverse(1, 1)
            split_hi(6, NX)
            roots(3)
            act.wait_ge(w_lo_pool, NX - N_DVE)
            act.wait_ge(w_lo_dve, N_DVE)
            attention_norm(3, 0)
            roots(4)
            attention_norm(4, 1)
            roots(5)
            normalise(5)
            roots(6)
            hi(0)
            hi(1)
            normalise(6)
            hi(2)
            logits_bias(0)
            hi(3)
            logits_bias(1)
            act.wait_ge(logits_ready, 1)
            act.activation(rt[:, 2], rt[:, 1], ACT.Exp).then_inc(exp_ready, 1)
            act.wait_ge(logits_ready, 2)
            act.activation(rs[:, 4], rs[:, 3], ACT.Exp).then_inc(exp_ready, 1)
            silu(0)
            silu(1)
            act_hi(0)
            silu(2)
            act_hi(1)
            silu(3)
            act_hi(2)
            y_odd(1)
            act_hi(3)
            y_odd(3)
            hi(FIRST)

            def step(p, i=0):
                if p + 2 < PAIRS or not isinstance(i, int):
                    hi(p + 2, i)
                if FIRST <= p < PAIRS:
                    silu(p, i)
                if FIRST <= p - 1 < PAIRS:
                    act_hi(p - 1, i)
                if FIRST <= p - 2 < PAIRS:
                    y_odd(p - 2, i)

            routed_steps(act, STEPS_BEFORE, step, STEPS_AFTER)
            act.preload_act_table_set("natural_log_exp_and_others")
            act.wait_ge(gates_ready, 1)

            def first_choices(o):
                act.wait_ge(yc_in[o], 16 * K)
                for j in range(o * OG, (o + 1) * OG):
                    act.activation(y_choice[0][:, j], y_choice[0][:, j], ACT.Copy, scale=gate_w[:, 0, j:j + 1]
                                   ).then_inc(first_weighted, 1)

            def output_norm(o):
                i, a = norm_order[6 + o]
                act.wait_ge(shift_ready, 5 + o)
                for j in range(a.start, a.stop):
                    act.activation(total[:, j], total[:, j], ACT.Identity, bias=ln_t[:, i, 6, j:j + 1],
                                   scale=ln_t[:, i, 5, j:j + 1]).then_inc(out_normed, 1)

            first_choices(0)
            first_choices(1)
            first_choices(2)
            for o in range(OUT_GROUPS):
                roots(7 + o)
                if o + 3 < OUT_GROUPS:
                    first_choices(o + 3)
                if o:
                    output_norm(o - 1)
            output_norm(OUT_GROUPS - 1)

        @block.vector
        def _(v):
            steps = [0]

            def chain(ins):
                steps[0] += 1
                ins.then_inc(v_chain, 1)
                v.wait_ge(v_chain, steps[0])

            def statistics(n, srcs, scale, eps):
                i, a = norm_order[n - 1]
                for j, src in zip(range(a.start, a.stop), srcs):
                    last = v.bn_stats(stats[:, j, :], src)
                chain(last)
                for j in range(a.start, a.stop):
                    last = v.bn_aggr(mv[:, i, j, :], stats[:, j, :])
                chain(last)
                v.tensor_scalar(ln_t[:, i, 0, a], mv[:, i, a, 1], scale, eps, ALU.mult, ALU.add).then_inc(var_ready, 1)

            def refine(n, want_shift=False):
                i, a = norm_order[n - 1]
                v.wait_ge(root_ready, n)
                chain(v.tensor_tensor(ln_t[:, i, 3, a], ln_t[:, i, 2, a], ln_t[:, i, 2, a], ALU.mult))
                chain(v.scalar_tensor_tensor(ln_t[:, i, 4, a], ln_t[:, i, 3, a], -0.5, ln_t[:, i, 0, a], ALU.mult, ALU.mult))
                chain(v.scalar_tensor_tensor(ln_t[:, i, 5, a], ln_t[:, i, 4, a], 1.5, ln_t[:, i, 2, a], ALU.add, ALU.mult))
                if want_shift:
                    v.scalar_tensor_tensor(ln_t[:, i, 6, a], mv[:, i, a, 0], -1.0, ln_t[:, i, 5, a], ALU.mult, ALU.mult).then_inc(shift_ready, 1)

            def normalise(n, src, dst, ready):
                i, a = norm_order[n - 1]
                for j in range(a.start, a.stop):
                    v.tensor_scalar(dst[:, j, 0:D], src[:, j], mv[:, i, j, 0:1], ln_t[:, i, 5, j:j + 1],
                                    ALU.subtract, ALU.mult).then_inc(ready, 1)

            for b in range(B):
                v.wait_ge(x_in[b], 16)
                statistics(b + 1, [x_tok[:, j] for j in range(b * JB, (b + 1) * JB)], 1.0 + LN_EPS, LN_EPS * LN_EPS)
                refine(b + 1)
                normalise(b + 1, x_tok, rows, hat_ready)
            v.wait_ge(col_in, 16)
            v.tensor_scalar(bias_s[:, 0], bqa, SCALE, None, ALU.mult).then_inc(bias_ready, 1)
            v.tensor_scalar(bias_s[:, 1], bka, SCALE, None, ALU.mult).then_inc(bias_ready, 1)

            v.tensor_copy(r_hi[:], wr).then_inc(r_split, 1)
            v.wait_ge(r_split, 1)
            v.tensor_tensor(r_lo[:], wr, r_hi[:].bitcast(F32), ALU.subtract).then_inc(r_split, 1)

            def split(first, last):
                for n in taken_by("dve")[first:last]:
                    e = expert_at(n)
                    v.wait_ge(stage_in[plan[n][0]], 16 * fills(n))
                    chain(v.tensor_copy(w_hi[:, e], stages[plan[n][0]]))
                    v.tensor_tensor(w_lo[:, e], stages[plan[n][0]], w_hi[:, e].bitcast(F32), ALU.subtract).then_inc(w_lo_dve, 1)

            def cumulate(which, b):
                for c in range(C):
                    n = which * U + b * C + c
                    a = slice(b * S, (b + 1) * S)
                    v.wait_ge(e_ready, n + 1)
                    v.tensor_tensor_scan(s_feat[:, c, a], e_feat[:, c, a], e_feat[:, c, a], 0.0, ALU.add, ALU.bypass).then_inc(sum_ready, 1)

            def pool_query(b, pair):
                a = slice(b * S, (b + 1) * S)
                for c in range(C):
                    n = b * C + c
                    v.wait_ge(inv_ready, n + 1)
                    v.wait_ge(eq_ready, n + 1)
                    chain(v.tensor_tensor(s_feat[:, c, a], q_feat[:, c, a], s_feat[:, c, a], ALU.mult))
                    chain(v.tensor_tensor_scan(p_feat[:, c, a], s_feat[:, c, a], s_feat[:, c, a], 0.0, ALU.add, ALU.bypass))
                    v.wait_ge(k_psum, n + 1)
                    v.scalar_tensor_tensor(m_feat[:, c, a], bank[ATT_BANKS[pair][c]][:], bk[:, c:c + 1], p_feat[:, c, a],
                                           ALU.add, ALU.mult).then_inc(mix_ready, 1)

            def pool_keys(b):
                a = slice(b * S, (b + 1) * S)
                for c in range(C):
                    n = b * C + c
                    v.wait_ge(inv_ready, U + n + 1)
                    v.wait_ge(eq_ready, U + n + 1)
                    chain(v.tensor_tensor(s_feat[:, c, a], m_feat[:, c, a], s_feat[:, c, a], ALU.mult))
                    chain(v.tensor_tensor_scan(p_feat[:, c, a], s_feat[:, c, a], s_feat[:, c, a], 0.0, ALU.add, ALU.bypass))

            def values(b, pair):
                a = slice(b * S, (b + 1) * S)
                for c in range(C):
                    v.wait_ge(v_psum, b * C + c + 1)
                    v.scalar_tensor_tensor(e_feat[:, c, a], bank[ATT_BANKS[pair][c]][:], bv[:, c:c + 1], p_feat[:, c, a],
                                           ALU.add, ALU.mult).then_inc(a_ready, 1)

            def att_rows(b, j):
                return bank[ATT_BANKS[2 * b][j // 2]][:, (j % 2) * D:(j % 2 + 1) * D]

            def att_statistics(n, b):
                v.wait_ge(aT_psum, 2 * b + 2)
                statistics(n, [att_rows(b, j) for j in range(JB)], 1.0, LN_EPS)

            def ffn_statistics(n, b):
                v.wait_ge(x1_ready, (b + 1) * JB)
                statistics(n, [x_tok[:, b * JB + j] for j in range(JB)], 1.0, LN_EPS)

            def lo(p, i=0):
                u, par = p % RING, p % 2
                v.wait_ge(hi_done, i + p + 1)
                if p >= FIRST:
                    v.tensor_copy(slot_row[:, bass.ds((i + (p - FIRST)) * 2, 2)], x_tiles[:, u, :, D].bitcast(U32)
                                  ).then_inc(row_nos_kept, 1)
                v.tensor_tensor(xl[:, u].rearrange("p t c s -> p (t c s)"), bank[2 + par][:],
                                xh[:, u].rearrange("p t c s -> p (t c s)").bitcast(F32), ALU.subtract).then_inc(lo_done, 1)

            def gated(p, i=0):
                par = p % 2
                v.wait_ge(silu_done, i + p + 1)
                if p >= 2:
                    v.wait_ge(a_done, i + p - 1)
                v.tensor_tensor(act_t[:, par], silu_t[:, par], bank[4 + par][:].rearrange("p (t g) -> p t g", t=2)[:, :, P:GU],
                                ALU.mult).then_inc(act_done, 1)

            def act_lo(p, i=0):
                par = p % 2
                v.wait_ge(ah_done, i + p + 1)
                v.tensor_tensor(al[:, par].rearrange("p t s -> p (t s)"), bank[6 + par][:, 0:2 * P],
                                ah[:, par].rearrange("p t s -> p (t s)").bitcast(F32), ALU.subtract).then_inc(al_done, 1)

            def y_even(p, i=0):
                if p % 2:
                    return
                u = p % RING
                v.wait_ge(d_done, i + p + 1)
                if p < SP_PAIRS:
                    v.tensor_copy(y_shared[:, 2 * p:2 * p + 2].rearrange("p t d -> p (t d)"), bank[0][:]).then_inc(y_done[0], 1)
                    return
                if p >= FIRST + RING:
                    v.wait_ge(y_out[u], 32 * ((p - FIRST) // RING) + i * (32 // RING))
                v.tensor_copy(y_tiles[:, u].rearrange("p t d -> p (t d)"), bank[0][:]).then_inc(y_done[0], 1)

            split(0, 4)
            cumulate(0, 0)
            pool_query(0, 1)
            split(4, 5)
            cumulate(0, 1)
            split(5, 6)
            pool_query(1, 3)
            cumulate(1, 0)
            split(6, 7)
            pool_keys(0)
            cumulate(1, 1)
            values(0, 2)
            pool_keys(1)
            values(1, 3)
            att_statistics(3, 0)
            refine(3, True)
            att_statistics(4, 1)
            refine(4, True)
            ffn_statistics(5, 0)
            refine(5, True)
            ffn_statistics(6, 1)
            refine(6, True)
            for p in range(SP_PAIRS):
                lo(p)

            def over_e(a):
                return a.rearrange("p (j o) -> p j o", o=1).to_broadcast([P, NJ, E])

            def over_j(a):
                return a.rearrange("p (o e) -> p o e", o=1).to_broadcast([P, NJ, E])

            v.wait_ge(logits_psum, B)
            logits = bank[0][:, 0:NJ * E].rearrange("p (j e) -> p j e", e=E)
            chain(v.tensor_reduce(rs[:, 0], logits, AX_X, ALU.max))
            chain(v.tensor_tensor(rt[:, 3], logits, over_e(rs[:, 0]), ALU.is_equal))
            v.tensor_tensor(rt[:, 1], logits, over_e(rs[:, 0]), ALU.subtract).then_inc(logits_ready, 1)
            chosen_k = rt[:, 8:10]
            for k in range(K):
                if k:
                    v.wait_ge(logits_ready, 1)
                    chain(v.scalar_tensor_tensor(rt[:, 5], chosen_k[:, 0], -3.0e38, rt[:, 1], ALU.mult, ALU.add))
                    v.tensor_reduce(rs[:, 3], rt[:, 5], AX_X, ALU.max).then_inc(logits_ready, 1)
                    v.wait_ge(logits_ready, 2)
                    chain(v.tensor_tensor(rt[:, 3], rt[:, 5], over_e(rs[:, 3]), ALU.is_equal))
                chain(v.tensor_tensor(rt[:, 4], rt[:, 3], over_j(rev_e), ALU.mult))
                chain(v.tensor_reduce(rs[:, 1 + k], rt[:, 4], AX_X, ALU.max))
                chain(v.tensor_tensor(chosen_k[:, k], rt[:, 4], over_e(rs[:, 1 + k]), ALU.is_equal))
            v.tensor_tensor(chosen[:], chosen_k[:, 0], chosen_k[:, 1], ALU.add).then_inc(chosen_ready, 1)
            chain(v.memset(before[:, 0:1], 0.0))
            v.wait_ge(rank_psum, 2)
            chain(v.tensor_scalar(ex[:, 0], bank[7][:, 256:256 + E], 1.0 / P, 0.5 - 0.5 / P, ALU.mult, ALU.add))
            chain(v.tensor_scalar(ex[:, 1], ex[:, 0], ROUND, -ROUND, ALU.add, ALU.add))
            chain(v.tensor_tensor_scan(before[:, 1:], ex[:, 1], ex[:, 1], 0.0, ALU.add, ALU.bypass))
            chain(v.scalar_tensor_tensor(rt[:, 10], over_j(before[:, 0:E]), float(P),
                                         bank[1][:, 0:NJ * E].rearrange("p (j e) -> p j e", e=E), ALU.mult, ALU.add))
            chain(v.tensor_tensor(rt[:, 6:8], chosen_k, rt[:, 10:11].to_broadcast([P, K, NJ, E]), ALU.mult))
            chain(v.tensor_reduce(rs[:, 8:10], rt[:, 6:8], AX_X, ALU.add))
            v.tensor_copy(slot_of[:], rs[:, 8:10]).then_inc(slot_ready, 1)
            chain(v.tensor_tensor(cmp[:], before[:, 1:].rearrange("p (o e) -> p o e", o=1).to_broadcast([P, TILES, E]),
                                  tile_no.rearrange("p (m o) -> p m o", o=1).to_broadcast([P, TILES, E]), ALU.is_le))
            chain(v.tensor_reduce(tile_e[:, 0], cmp[:], AX_X, ALU.add))
            v.tensor_scalar(tile_e_i[:], tile_e[0:1, 0], float(E - 1), None, ALU.min).then_inc(tile_e_ready, 1)
            v.wait_ge(exp_ready, 2)
            chain(v.tensor_reduce(rs[:, 5], rt[:, 2], AX_X, ALU.add))
            chain(v.scalar_tensor_tensor(rs[:, 6], rs[:, 5], TOPK_EPS, rs[:, 4], ALU.mult, ALU.add))
            chain(v.tensor_scalar(rs[:, 7], rs[:, 6], 1.0, None, ALU.add))
            chain(v.reciprocal(gate_w[:, 0], rs[:, 7]))
            v.tensor_tensor(gate_w[:, 1], gate_w[:, 0], rs[:, 4], ALU.mult).then_inc(gates_ready, 1)
            gated(0)
            gated(1)
            act_lo(0)
            gated(2)
            act_lo(1)
            y_even(0)
            gated(3)
            act_lo(2)
            act_lo(3)
            y_even(2)
            lo(FIRST)

            def step(p, i=0):
                if p + 2 < PAIRS or not isinstance(i, int):
                    lo(p + 2, i)
                if FIRST <= p < PAIRS:
                    gated(p, i)
                if FIRST <= p - 1 < PAIRS:
                    act_lo(p - 1, i)
                if FIRST <= p - 2 < PAIRS:
                    y_even(p - 2, i)

            routed_steps(v, STEPS_BEFORE, step, STEPS_AFTER)

            v.wait_ge(y_done[1], PAIRS // 2)
            def experts_sum(o):
                for j in range(o * OG, (o + 1) * OG):
                    v.wait_ge(first_and_shared, j + 1)
                    last = v.scalar_tensor_tensor(total[:, j], y_choice[1][:, j], gate_w[:, 1, j:j + 1], y_choice[0][:, j],
                                                  ALU.mult, ALU.add)
                chain(last)
                statistics(7 + o, [total[:, j] for j in range(o * OG, (o + 1) * OG)], 1.0, LN_EPS)

            experts_sum(0)
            for o in range(OUT_GROUPS):
                if o + 1 < OUT_GROUPS:
                    experts_sum(o + 1)
                refine(7 + o, True)
            add_x1(v, range(OUT_GROUPS - 1, OUT_GROUPS))

        @block.gpsimd
        def _(g):
            g.memset(ident[:], 0.0).then_inc(consts, 1)
            g.memset(pad_row[:], 0.0).then_inc(pad_made, 1)
            g.memset(earlier[:], 1.0).then_inc(consts, 1)
            g.memset(ones_bf[:], 1.0).then_inc(consts, 1)
            g.wait_ge(consts, 3)
            g.affine_select(out=ident[:], in_=ident[:], compare_op=ALU.not_equal, fill=1.0, base=0,
                            pattern=[[-1, P]], channel_multiplier=1).then_inc(consts2, 1)
            g.affine_select(out=earlier[:], in_=earlier[:], compare_op=ALU.is_gt, fill=0.0, base=0,
                            pattern=[[1, P]], channel_multiplier=-1).then_inc(consts2, 1)
            g.wait_ge(pad_made, 1)
            g.iota(pad_row[:, D:ROW].bitcast(I32), [[1, 1]], base=NO_ROW, channel_multiplier=0).then_inc(pad_made, 1)
            g.iota(idx_i[:, 0:E], [[-1, E]], base=E, channel_multiplier=0).then_inc(consts, 1)
            g.iota(idx_i[:, E:E + TILES], [[1, TILES]], base=0, channel_multiplier=0).then_inc(consts, 1)
            g.iota(row_no[:], [[T, K], [P, NJ]], base=0, channel_multiplier=1).then_inc(row_nos, 1)
            g.wait_ge(consts, 5)
            g.tensor_copy(idx_f[:], idx_i[:]).then_inc(consts2, 1)

            pool_experts = taken_by("pool")

            def split_lo(first, last):
                for i, n in list(enumerate(pool_experts))[first:last]:
                    e = expert_at(n)
                    g.wait_ge(w_hi_act, i + 1)
                    g.tensor_tensor(w_lo[:, e], stages[plan[n][0]], w_hi[:, e].bitcast(F32), ALU.subtract).then_inc(w_lo_pool, 1)

            def weighted(which, b):
                src = m_feat if which else q_feat
                for c in range(C):
                    a = slice(b * S, (b + 1) * S)
                    g.wait_ge(e_ready, which * U + b * C + c + 1)
                    if not which:
                        g.wait_ge(qa_psum, (b + 1) * C)
                    else:
                        g.wait_ge(ka_psum, (b + 1) * C)
                    g.tensor_tensor(src[:, c, a], e_feat[:, c, a], src[:, c, a], ALU.mult).then_inc(eq_ready, 1)

            split_lo(0, 1)
            weighted(0, 0)
            split_lo(1, 3)
            weighted(0, 1)
            split_lo(3, 5)
            weighted(1, 0)
            weighted(1, 1)
            split_lo(5, NX)
            for j in range(NJ):
                g.wait_ge(att_ready, j + 1)
                g.tensor_tensor(x_tok[:, j], rows[:, j, 0:D], x_tok[:, j], ALU.add).then_inc(x1_ready, 1)
            g.wait_ge(row_nos, 1)
            g.wait_ge(pad_out, 16)
            g.wait_ge(slot_ready, 1)
            for k in range(K):
                for b in range(B):
                    if k:
                        g.wait_ge(rows_out[k - 1][b], 16 * JB)
                    half = slice(b * JB, (b + 1) * JB)
                    g.tensor_copy(rows[:, half, D].bitcast(I32), row_no[:, k, half]).then_inc(id_ready, 1)
                    g.wait_ge(id_ready, k * B + b + 1)
                    for j in range(b * JB, (b + 1) * JB):
                        g.indirect_dma_start(out=slots, out_offset=bass.IndirectOffsetOnAxis(slot_of[:, k, j:j + 1], 0),
                                             in_=rows[:, j, :], in_offset=None).then_inc(rows_out[k][b], 16)

            for p in range(FIRST, PAIRS):
                g.wait_ge(row_nos_kept, p - FIRST + 1)
                g.wait_ge(y_done[p % 2], p // 2 + 1)
                for t in range(2):
                    m = (p - FIRST) * 2 + t
                    g.indirect_dma_start(out=routed, out_offset=bass.IndirectOffsetOnAxis(slot_row[:, m:m + 1], 0),
                                         in_=y_tiles[:, p % RING, t], in_offset=None, bounds_check=K * T - 1,
                                         oob_is_err=False).then_inc(y_out[p % RING], 16)
            g.wait_ge(y_done[0], PAIRS // 2)
            g.wait_ge(y_done[1], PAIRS // 2)
            def add_shared(o):
                for j in range(o * OG, (o + 1) * OG):
                    g.wait_ge(first_weighted, j + 1)
                    g.tensor_tensor(y_choice[0][:, j], y_choice[0][:, j], y_shared[:, j], ALU.add).then_inc(first_and_shared, 1)

            for o in range(OUT_GROUPS):
                add_shared(o)
            add_x1(g, range(OUT_GROUPS - 1))


def kernel(**inputs):
    import numpy as np
    import concourse.bacc as bacc
    from concourse.bass_utils import run_bass_kernel_spmd

    a = {n: np.asarray(v) for n, v in inputs.items()}
    x = np.ascontiguousarray(a["L0_attn_hidden_states"])
    D = x.shape[2]
    C = D // P
    attn_w = np.stack([a["L0_attn_" + n].T.reshape(C, P, D) for n in ("Wq", "Wqa", "Wk", "Wka", "Wv")])
    attn_w = np.ascontiguousarray(attn_w.transpose(2, 0, 1, 3))
    cols = np.stack([a["L0_attn_" + n].reshape(C, P) for n in ("ln_g", "ln_b", "bq", "bqa", "bk", "bka", "bv")])
    wr = a["L0_ffn_Wr"].T.reshape(C, P, -1)
    E = wr.shape[2]
    bias = np.zeros((P, 1), x.dtype)
    bias[:E, 0] = a["L0_ffn_bias"].reshape(-1)
    misc = np.concatenate([cols.transpose(2, 0, 1).reshape(P, -1), wr.transpose(1, 0, 2).reshape(P, -1),
                           bias], axis=1)
    misc = np.ascontiguousarray(misc)
    wg = np.concatenate([a["L0_ffn_Wg"], a["L0_ffn_sWg"][None]])
    wu = np.concatenate([a["L0_ffn_Wu"], a["L0_ffn_sWu"][None]])
    wd = np.concatenate([a["L0_ffn_Wd"], a["L0_ffn_sWd"][None]])
    gu = np.concatenate([wg, wu], axis=2).reshape(E + 1, C, P, -1).transpose(2, 0, 1, 3).reshape(P, E + 1, -1)
    expert_w = np.ascontiguousarray(np.concatenate([gu, wd.transpose(1, 0, 2)], axis=2))

    nc = bacc.Bacc("TRN2", target_bir_lowering=False, num_devices=1)
    arrays = {"x": x, "attn_w": attn_w, "misc": misc, "expert_w": expert_w}
    args = [nc.dram_tensor(n, v.shape, mybir.dt.from_np(v.dtype), kind="ExternalInput").ap() for n, v in arrays.items()]
    out = nc.dram_tensor("out", x.shape, F32, kind="ExternalOutput").ap()
    block_kernel(nc, *args, out)
    r = run_bass_kernel_spmd(nc, [arrays], core_ids=[0])
    return r.results[0]["out"]
```

```python
from contextlib import ExitStack

import concourse.bass as bass
from concourse import mybir

F32 = mybir.dt.float32
F32R = mybir.dt.float32r
BF16 = mybir.dt.bfloat16
I32 = mybir.dt.int32
U32 = mybir.dt.uint32
ALU = mybir.AluOpType
ACT = mybir.ActivationFunctionType
AX_X = mybir.AxisListType.X

P = 128
LN_EPS = 1e-5
TOPK_EPS = 1e-9


def block_kernel(nc, x, attn_w, misc, expert_w, out):
    B, S, D = x.shape
    T = B * S
    C = D // P
    NJ = T // P
    JB = S // P
    _, NX, EW = expert_w.shape
    E = NX - 1
    GU = 2 * P
    NCOL = 7
    K = 2
    TILES_MAX = (K * T) // P + E - 1
    TILES = TILES_MAX + TILES_MAX % 2
    SP_PAIRS = NJ // 2
    PAIRS = SP_PAIRS + TILES // 2
    RING = 4
    U = B * C
    SCALE = 1.0 / float(D) ** 0.5
    WARM_START, WARM_FIRST, WARM_UP, WARM_ROUTER, WARM_TOKENS, WARM_GATHER, WARM_GATHERED = 20, 5, 9, 7, 11, 4, 5
    GROUP = (NJ - 2) // 2
    OUT_GROUPS = [slice(0, GROUP), slice(GROUP, NJ - 2), slice(NJ - 2, NJ)]
    X1_DVE = JB - 1
    XN_DVE = (1, 2)
    POOL_GROUP = 1
    ROUND = 1.5 * 2.0 ** 23
    assert (TILES % 2, NJ % 2, (PAIRS - SP_PAIRS) % RING, SP_PAIRS % RING) == (0, 0, 0, 0)

    normed = nc.dram_tensor("normed", (T, D), F32).ap()
    y_slots = nc.dram_tensor("y_slots", (TILES * P, D), F32).ap()

    with ExitStack() as ctx:
        def sb(name, shape, dt=F32):
            return ctx.enter_context(nc.sbuf_tensor(name, shape, dt))

        def sem(name):
            return ctx.enter_context(nc.semaphore(name))

        bank = [ctx.enter_context(nc.psum_tensor(f"bank{i}", [P, 512], F32)) for i in range(8)]

        x_tok = sb("x_tok", [P, NJ, D])
        rows = sb("rows", [P, NJ, D])
        h_feat = sb("h_feat", [P, C, T])
        q_feat = sb("q_feat", [P, C, T])
        e_feat = sb("e_feat", [P, C, T])
        s_feat = sb("s_feat", [P, C, T])
        p_feat = sb("p_feat", [P, C, T])
        m_feat = sb("m_feat", [P, C, T])
        w_attn = sb("w_attn", [P, 5, C, D])
        col = sb("col", [P, NCOL * C + C * E + 1])
        bias_s = sb("bias_s", [P, 2, C])
        w_stage = sb("w_stage", [P, 2, EW])
        row_halves = rows[:].rearrange("p (b j) d -> p b (j d)", b=B)
        stages = [w_stage[:, 0], w_stage[:, 1], row_halves[:, 0, 0:EW], row_halves[:, 1, 0:EW]]
        w_hi = sb("w_hi", [P, NX, EW], F32R)
        w_lo = sb("w_lo", [P, NX, EW], F32R)
        r_hi = sb("r_hi", [P, C, E], F32R)
        r_lo = sb("r_lo", [P, C, E], F32R)
        xh = sb("xh", [P, RING, 2, C, P], F32R)
        xl = sb("xl", [P, RING, 2, C, P], F32R)
        ah = sb("ah", [P, 2, 2, P], F32R)
        al = sb("al", [P, 2, 2, P], F32R)
        x_tiles = s_feat[:].rearrange("p c (r d) -> p (c r) d", d=2 * D).rearrange("p r (t d) -> p r t d", t=2)
        y_tiles = p_feat[:].rearrange("p c (r d) -> p (c r) d", d=2 * D).rearrange("p r (t d) -> p r t d", t=2)
        y_shared = q_feat[:].rearrange("p c (j d) -> p (c j) d", d=D)
        y_choice = [h_feat[:].rearrange("p c (j d) -> p (c j) d", d=D),
                    m_feat[:].rearrange("p c (j d) -> p (c j) d", d=D)]
        act_t = w_attn[:, 0].rearrange("p c (t i) -> p c t i", t=2)
        silu_t = w_attn[:, 1].rearrange("p c (t i) -> p c t i", t=2)
        total = s_feat[:].rearrange("p c (j d) -> p (c j) d", d=D)
        result = e_feat[:].rearrange("p c (j d) -> p (c j) d", d=D)
        logits_t = m_feat[0:E, 0]
        ident = sb("ident", [P, P])
        earlier = sb("earlier", [P, P], BF16)
        ones_bf = sb("ones_bf", [P, P], BF16)
        N_IDX = E + TILES + P + K * NJ + 1
        idx_i = sb("idx_i", [P, N_IDX], I32)
        idx_f = sb("idx_f", [P, N_IDX])
        pos_no = sb("pos_no", [P, P], BF16)
        rev_e, tile_no = idx_f[:, 0:E], idx_f[:, E:E + TILES]
        tok_hi = idx_f[:, E + TILES + P:N_IDX - 1]
        tok_lo = idx_f[:, N_IDX - 1:]
        stats = sb("stats", [P, NJ, 6])
        mv = sb("mv", [P, 4, NJ, 2])
        ln_t = sb("ln_t", [P, 4, 7, NJ])
        router = p_feat[:].rearrange("p c t -> p (c t)")
        rt = router[:, 0:12 * NJ * E].rearrange("p (n j e) -> p n j e", j=NJ, e=E)
        cmp = router[:, 12 * NJ * E:].rearrange("p (m e) -> p m e", e=E)
        chosen = sb("chosen", [P, NJ, E], BF16)
        warm_rows = ones_bf[:].rearrange("p (o i) -> p o i", o=1).to_broadcast([P, 4, P])
        rs = w_attn[:, 2, 1, 0:16 * NJ].rearrange("p (n j) -> p n j", j=NJ)
        ex = w_attn[:, 2, 1, 16 * NJ:16 * NJ + 4 * E].rearrange("p (n e) -> p n e", e=E)
        diff_e, exp_e = (w_attn[:, 3, c, 0:NJ * E].rearrange("p (j e) -> p j e", e=E) for c in range(2))
        before = w_attn[:, 2, 0, 4 * TILES:4 * TILES + E + 1]
        tile_e = w_attn[:, 2, 0, 0:4 * TILES].rearrange("p (n m) -> p n m", m=TILES)
        tile_e_i = sb("tile_e_i", [1, TILES], I32)
        slot_of = sb("slot_of", [P, K, NJ], U32)
        gate_w = sb("gate_w", [P, K, NJ])
        token_of = sb("token_of", [P, TILES], U32)
        KJ = K * NJ
        one_hots = w_stage[:].rearrange("p s n -> p (s n)").bitcast(BF16)
        pos_hot = one_hots[:, 0:KJ * P].rearrange("p (n s) -> p n s", s=P)
        tile_lo = one_hots[:, KJ * P:KJ * (P + TILES)].rearrange("p (n m) -> p n m", m=TILES)
        tile_hi = one_hots[:, KJ * (P + TILES):KJ * (P + 2 * TILES)].rearrange("p (n m) -> p n m", m=TILES)
        tile_hot = e_feat[:, 0, 0:KJ * TILES].rearrange("p (n m) -> p n m", m=TILES)
        assert KJ * (P + 2 * TILES) <= 4 * EW

        g_col, b_col, bq, bqa, bk, bka, bv = [col[:, i * C:(i + 1) * C] for i in range(NCOL)]
        wr = col[:, NCOL * C:NCOL * C + C * E].rearrange("p (c e) -> p c e", c=C)
        r_bias = col[0:E, NCOL * C + C * E:]
        WQ, WQA, WK, WKA, WV = range(5)

        x_in = [sem(f"x_in{h}") for h in range(2 * B)]
        col_in, wq_in, wqk_in, wrest_in = sem("col_in"), sem("wq_in"), sem("wqk_in"), sem("wrest_in")
        stage_in = [sem(f"stage_in{i}") for i in range(4)]
        consts, consts2 = sem("consts"), sem("consts2")
        v_chain = sem("v_chain")
        var_ready, root_ln, root_ready = (sem(n) for n in ("var_ready", "root_ln", "root_ready"))
        shift_ready, out_normed = sem("shift_ready"), sem("out_normed")
        first_added = sem("first_added")
        total_ready, last_normed = sem("total_ready"), sem("last_normed")
        hat_ready = sem("hat_ready")
        hT_psum, hT_ready = sem("hT_psum"), sem("hT_ready")
        q_psum, q_ready = sem("q_psum"), sem("q_ready")
        qa_psum, e_ready, sum_ready, log_ready, inv_ready = (sem(n) for n in ("qa_psum", "e_ready", "sum_ready", "log_ready", "inv_ready"))
        eq_ready, k_psum, mix_ready, v_psum, a_ready = (sem(n) for n in ("eq_ready", "k_psum", "mix_ready", "v_psum", "a_ready"))
        ka_psum = sem("ka_psum")
        w_hi_act = sem("w_hi_act")
        r_split, logits_t_psum, logits_t_ready = sem("r_split"), sem("logits_t_psum"), sem("logits_t_ready")
        w_lo_pool, w_lo_dve = sem("w_lo_pool"), sem("w_lo_dve")
        bias_ready = sem("bias_ready")
        aT_psum, att_ready, x1_ready, xn_ready = sem("aT_psum"), sem("att_ready"), sem("x1_ready"), sem("xn_ready")
        x1_dve = sem("x1_dve")
        xn_dve = sem("xn_dve")
        logits_psum, logits_ready, exp_ready = sem("logits_psum"), sem("logits_ready"), sem("exp_ready")
        chosen_ready, rank_psum, slot_ready, tile_e_ready = (sem(n) for n in ("chosen_ready", "rank_psum", "slot_ready", "tile_e_ready"))
        gates_ready, normed_out = sem("gates_ready"), sem("normed_out")
        tile_hot_ready, pos_hot_ready, tile_lo_ready, tile_hi_ready, token_psum, token_ready = (
            sem(n) for n in ("tile_hot_ready", "pos_hot_ready", "tile_lo_ready", "tile_hi_ready", "token_psum", "token_ready"))
        xt_in = [sem(f"xt_in{u}") for u in range(RING)]
        t_done, hi_done, lo_done, gu_done, silu_done, act_done = (sem(n) for n in ("t_done", "hi_done", "lo_done", "gu_done", "silu_done", "act_done"))
        a_done, ah_done, al_done, d_done = (sem(n) for n in ("a_done", "ah_done", "al_done", "d_done"))
        y_done = [sem("y_done_even"), sem("y_done_odd")]
        y_out = [sem(f"y_out{u}") for u in range(RING)]
        yc_in = [[sem(f"yc_in{k}_{j}") for j in range(NJ)] for k in range(K)]
        o_ready, o_out = [sem(f"o_ready{o}") for o in range(len(OUT_GROUPS))], sem("o_out")

        DVE, POOL = "dve", "pool"
        plan = [(0, POOL), (1, POOL), (2, DVE), (0, DVE), (1, DVE), (2, POOL), (3, POOL), (0, POOL), (1, DVE),
                (2, POOL), (3, POOL), (0, POOL), (1, DVE), (2, POOL), (3, POOL), (0, POOL), (1, POOL)]
        N_DVE = sum(who == DVE for _, who in plan)

        def expert_at(n):
            return (n - 1) % NX

        def fills(n):
            return sum(plan[m][0] == plan[n][0] for m in range(n + 1))

        def taken_by(who):
            return [n for n in range(NX) if plan[n][1] == who]

        def wait_stage_free(engine, n):
            last = [m for m in range(n) if plan[m][0] == plan[n][0]]
            if last:
                who = plan[last[-1]][1]
                engine.wait_ge(w_lo_dve if who == DVE else w_lo_pool, taken_by(who).index(last[-1]) + 1)

        def tok_tiles(dram, j0, n):
            return dram.rearrange("(j p) d -> p j d", p=P)[:, j0:j0 + n, :]

        x_rows = x.rearrange("b s d -> (b s) d")
        out_rows = out.rearrange("b s d -> (b s) d")
        ATT_BANKS = [(0, 1), (2, 3), (4, 5), (6, 7)]

        def routed_steps(engine, before, body, after):
            for p in before:
                body(p)
            loops, rest = divmod(after[0] - before[-1] - 1, RING)
            assert rest == 0
            with engine.Fori(0, loops, 1) as i:
                for u in range(RING):
                    body(before[-1] + 1 + u, i * RING)
            for p in after:
                body(p)

        FIRST = SP_PAIRS
        STEPS_BEFORE = range(FIRST - 1, FIRST + 6)
        STEPS_AFTER = range(PAIRS - 2, PAIRS + 2)

        N_IN, N_ATT, N_FFN, N_OUT = range(4)
        norm_order = [(i, slice(b * JB, (b + 1) * JB)) for i, b in
                      ((N_IN, 0), (N_IN, 1), (N_ATT, 0), (N_ATT, 1), (N_FFN, 0), (N_FFN, 1))]
        norm_order += [(N_OUT, a) for a in OUT_GROUPS]

        def add_x1(engine, o):
            for j in range(OUT_GROUPS[o].start, OUT_GROUPS[o].stop):
                if j == NJ - 1:
                    engine.wait_ge(last_normed, 1)
                else:
                    engine.wait_ge(out_normed, j + 1)
                engine.tensor_tensor(result[:, j], total[:, j], x_tok[:, j], ALU.add).then_inc(o_ready[o], 1)

        block = ctx.enter_context(nc.Block())

        @block.sync
        def _(sp):
            JH = JB // 2

            def load_x(h):
                sp.dma_start(x_tok[:, h * JH:(h + 1) * JH], tok_tiles(x_rows, h * JH, JH)).then_inc(x_in[h], 16)

            load_x(0)
            load_x(1)
            sp.dma_start(col[:], misc).then_inc(col_in, 16)
            sp.dma_start(w_attn[:, 0:1], attn_w[:, 0:1]).then_inc(wq_in, 16)
            for h in range(2, 2 * B):
                load_x(h)
            sp.dma_start(w_attn[:, 1:3], attn_w[:, 1:3]).then_inc(wqk_in, 16)
            for n in range(NX):
                stage = plan[n][0]
                if stage >= 2 and fills(n) == 1:
                    sp.wait_ge(hT_psum, (stage - 1) * C)
                wait_stage_free(sp, n)
                sp.dma_start(stages[stage], expert_w[:, expert_at(n)]).then_inc(stage_in[stage], 16)
                if n == 3:
                    sp.dma_start(w_attn[:, 3:5], attn_w[:, 3:5]).then_inc(wrest_in, 16)
            for b in range(B):
                sp.wait_ge(xn_ready, (b + 1) * JB // 2)
                sp.wait_ge(xn_dve, (b + 1) * JB // 2)
                sp.dma_start(tok_tiles(normed, b * JB, JB), rows[:, b * JB:(b + 1) * JB]).then_inc(normed_out, 16)

            def store(p, i=0):
                sp.wait_ge(y_done[p % 2], i // 2 + p // 2 + 1)
                sp.dma_start(y_slots.rearrange("(m t p) d -> m p t d", p=P, t=2)[bass.ds(i + p - FIRST, 1)]
                             .rearrange("o p t d -> (o p) t d"), y_tiles[:, p % RING]).then_inc(y_out[p % RING], 16)

            with sp.Fori(0, (PAIRS - FIRST) // RING, 1) as i:
                for u in range(RING):
                    store(FIRST + u, i * RING)
            for o, a in enumerate(OUT_GROUPS):
                sp.wait_ge(o_ready[o], a.stop - a.start)
                sp.dma_start(tok_tiles(out_rows, a.start, a.stop - a.start), result[:, a]).then_inc(o_out, 16)
            sp.wait_ge(o_out, 16 * len(OUT_GROUPS))

        @block.tensor
        def _(pe):
            def att_bank(pair, c):
                return bank[ATT_BANKS[pair][c]]

            def transposed(pair, b):
                for j in range(JB):
                    pe.wait_ge(hat_ready, b * JB + j + 1)
                    for c in range(C):
                        last = pe.transpose(att_bank(pair, c)[:, j * P:(j + 1) * P],
                                            rows[:, b * JB + j, c * P:(c + 1) * P], ident[:])
                        if j == JB - 1:
                            last.then_inc(hT_psum, 1)

            def project(w, src, ready, pair, b, done):
                for ic in range(C):
                    pe.wait_ge(ready, b * C + ic + 1)
                    for oc in range(C):
                        last = pe.matmul(att_bank(pair, oc)[:], w_attn[:, w, ic, oc * P:(oc + 1) * P],
                                         src[:, ic, b * S:(b + 1) * S], start=ic == 0, stop=ic == C - 1)
                        if ic == C - 1:
                            last.then_inc(done, 1)

            def keep_warm(n, unused=bank[7]):
                for _ in range(n):
                    pe.matmul(unused[:], ones_bf[:], warm_rows, start=True, stop=True)

            pe.wait_ge(consts2, 2)
            keep_warm(WARM_START)
            transposed(0, 0)
            keep_warm(WARM_FIRST)
            pe.wait_ge(wq_in, 16)
            project(WQ, h_feat, hT_ready, 2, 0, q_psum)
            transposed(1, 1)
            pe.wait_ge(wqk_in, 16)
            project(WQA, q_feat, q_ready, 0, 0, qa_psum)
            pe.wait_ge(hT_ready, 2 * C)
            project(WK, h_feat, hT_ready, 1, 0, k_psum)
            project(WQ, h_feat, hT_ready, 3, 1, q_psum)
            project(WQA, q_feat, q_ready, 2, 1, qa_psum)
            pe.wait_ge(q_ready, 2 * C)
            project(WK, h_feat, hT_ready, 3, 1, k_psum)
            pe.wait_ge(wrest_in, 16)
            pe.wait_ge(e_ready, C)
            project(WKA, m_feat, mix_ready, 0, 0, ka_psum)
            pe.wait_ge(mix_ready, C)
            project(WKA, m_feat, mix_ready, 1, 1, ka_psum)
            pe.wait_ge(e_ready, U)
            project(WV, h_feat, hT_ready, 2, 0, v_psum)
            pe.wait_ge(mix_ready, 2 * C)
            project(WV, h_feat, hT_ready, 3, 1, v_psum)

            def att_transposed(b, pair):
                pe.wait_ge(a_ready, (b + 1) * C)
                pe.wait_ge(e_ready, U + (b + 1) * C)
                for j in range(JB):
                    for c in range(C):
                        last = pe.transpose(bank[ATT_BANKS[pair][j // 2]][:, (j % 2) * D + c * P:(j % 2) * D + (c + 1) * P],
                                            e_feat[:, c, b * S + j * P:b * S + (j + 1) * P], ident[:])
                    if j % 2:
                        last.then_inc(aT_psum, 1)

            att_transposed(0, 0)
            att_transposed(1, 2)

            def tiles(p):
                return range(1) if (p - FIRST) * 2 + 1 == TILES_MAX else range(2)

            def turn(p, i=0):
                u, par = p % RING, p % 2
                if p < SP_PAIRS:
                    pe.wait_ge(xn_dve if p in XN_DVE else xn_ready, (p // 2 + 1) * JB // 2)
                else:
                    pe.wait_ge(xt_in[u], 32 * ((p - FIRST) // RING + 1) + i * (32 // RING))
                if p >= 2:
                    pe.wait_ge(lo_done, i + p - 1)
                for t in tiles(p):
                    for c in range(C):
                        src = rows[:, 2 * p + t, c * P:(c + 1) * P] if p < SP_PAIRS else x_tiles[:, u, t, c * P:(c + 1) * P]
                        last = pe.transpose(bank[2 + par][:, (t * C + c) * P:(t * C + c + 1) * P], src, ident[:])
                last.then_inc(t_done, 1)

            def gate_up(p, i=0):
                u, par = p % RING, p % 2
                experts = tile_experts(p)
                pe.wait_ge(lo_done, i + p + 1)
                if p >= 2:
                    pe.wait_ge(act_done, i + p - 1)
                for t in tiles(p):
                    dst = bank[4 + par][:, t * GU:(t + 1) * GU]
                    parts = [(a, w, c) for c in range(C) for a, w in ((xh, w_hi), (xh, w_lo))] + [(xl, w_hi, c) for c in range(C)]
                    for n, (a, w, c) in enumerate(parts):
                        last = pe.matmul(dst, a[:, u, t, c, :], w[:, bass.ds(experts[t], 1), c * GU:(c + 1) * GU],
                                         start=n == 0, stop=n == len(parts) - 1)
                last.then_inc(gu_done, 1)

            def turn_act(p, i=0):
                par = p % 2
                pe.wait_ge(act_done, i + p + 1)
                if p >= 2:
                    pe.wait_ge(al_done, i + p - 1)
                for t in tiles(p):
                    last = pe.transpose(bank[6 + par][:, t * P:(t + 1) * P], act_t[:, par, t, :], ident[:])
                last.then_inc(a_done, 1)

            def down(p, i=0):
                par = p % 2
                experts = tile_experts(p)
                pe.wait_ge(al_done, i + p + 1)
                if p >= 2:
                    pe.wait_ge(y_done[par], i // 2 + p // 2)
                for t in tiles(p):
                    dst = bank[par][:, t * D:(t + 1) * D]
                    parts = ((ah, w_hi), (ah, w_lo), (al, w_hi))
                    for n, (a, w) in enumerate(parts):
                        last = pe.matmul(dst, a[:, par, t, :], w[:, bass.ds(experts[t], 1), C * GU:C * GU + D],
                                         start=n == 0, stop=n == len(parts) - 1)
                last.then_inc(d_done, 1)

            expert_reg = [[pe.alloc_register(f"expert_{u}_{t}") for t in range(2)] for u in range(RING)]

            def load_experts(p, i=0):
                pe.load(expert_reg[p % RING], tile_e_i[0:1, bass.ds((i + (p - FIRST)) * 2, 2)])

            def tile_experts(p):
                if p < SP_PAIRS:
                    return E, E
                return [nc.s_assert_within(pe.snap(r), 0, E - 1, skip_runtime_bounds_check_because="a minimum with E - 1 wrote it")
                        for r in expert_reg[p % RING]]

            def logits(b):
                pe.wait_ge(lo_done, 2 * b + 2)
                parts = [(a, w, c) for c in range(C) for a, w in ((xh, r_hi), (xh, r_lo), (xl, r_hi))]
                for n, (a, w, c) in enumerate(parts):
                    last = pe.matmul(bank[6 + b][0:E, :], w[:, c, :], a[:, 2 * b:2 * b + 2, :, c, :].rearrange("e p t s -> e (p t) s"),
                                     start=n == 0, stop=n == len(parts) - 1)
                last.then_inc(logits_t_psum, 1)

            def logits_by_token(b):
                pe.wait_ge(logits_t_ready, b + 1)
                for j in range(b * JB, (b + 1) * JB):
                    last = pe.transpose(bank[0][:, j * E:(j + 1) * E], logits_t[:, j * P:(j + 1) * P], ident[0:E, 0:E])
                last.then_inc(logits_psum, 1)

            pe.wait_ge(r_split, 2)
            pe.wait_ge(x1_ready, JB - 1)
            pe.wait_ge(x1_dve, 1)
            keep_warm(WARM_UP)
            turn(0)
            turn(1)
            keep_warm(WARM_ROUTER)
            turn(2)
            turn(3)
            logits(0)
            logits(1)
            logits_by_token(0)
            logits_by_token(1)
            pe.wait_ge(x1_ready, NJ - 1)
            pe.wait_ge(w_lo_pool, 1)
            gate_up(0)
            gate_up(1)
            pe.wait_ge(chosen_ready, 1)
            flat = chosen[:].rearrange("p j e -> p (j e)")
            pe.matmul(bank[1][:, 0:NJ * E], earlier[:], flat, start=True, stop=False, skip_group_check=True)
            for j in range(1, NJ):
                last = pe.matmul(bank[1][:, j * E:NJ * E], ones_bf[:], flat[:, 0:(NJ - j) * E], start=False, stop=j == NJ - 1,
                                 skip_group_check=True)
            last.then_inc(rank_psum, 1)
            for j in range(NJ):
                last = pe.matmul(bank[7][:, 256:256 + E], ones_bf[:], chosen[:, j, :], start=j == 0, stop=j == NJ - 1)
            last.then_inc(rank_psum, 1)
            turn_act(0)
            gate_up(2)
            keep_warm(WARM_TOKENS, bank[0])
            pe.wait_ge(tile_lo_ready, 1)
            pe.wait_ge(tile_hi_ready, 1)
            for n in range(KJ):
                pe.wait_ge(pos_hot_ready, n + 1)
                for m, part in enumerate((tile_lo, tile_hi)):
                    last = pe.matmul(bank[1][:, 256:256 + TILES], pos_hot[:, n], part[:, n], start=n + m == 0,
                                     stop=n == KJ - 1 and m == 1)
            last.then_inc(token_psum, 1)
            gate_up(3)
            pe.wait_ge(token_ready, 1)
            pe.wait_ge(slot_ready, 1)
            turn_act(1)
            down(0)
            turn_act(2)
            down(1)
            pe.wait_ge(w_lo_dve, N_DVE)
            pe.wait_ge(w_lo_pool, NX - N_DVE)
            keep_warm(WARM_GATHER)
            turn(FIRST)
            keep_warm(WARM_GATHERED)
            pe.wait_ge(tile_e_ready, 1)
            load_experts(FIRST)

            def step(p, i=0):
                if FIRST <= p < PAIRS:
                    gate_up(p, i)
                if FIRST <= p + 1 < PAIRS and p >= FIRST:
                    load_experts(p + 1, i)
                if FIRST <= p < PAIRS:
                    down(p - 2, i)
                if FIRST <= p < PAIRS + 1:
                    turn_act(p - 1, i)
                if PAIRS <= p:
                    down(p - 2, i)
                if p + 2 < PAIRS or not isinstance(i, int):
                    turn(p + 2, i)

            routed_steps(pe, STEPS_BEFORE, step, STEPS_AFTER)

        @block.scalar
        def _(act):
            act.preload_act_table_set("natural_log_exp_and_others")

            def roots(n):
                act.wait_ge(var_ready, n)
                i, a = norm_order[n - 1]
                act.activation(ln_t[:, i, 1, a], ln_t[:, i, 0, a], ACT.Ln).then_inc(root_ln, 1)
                act.wait_ge(root_ln, n)
                act.activation(ln_t[:, i, 2, a], ln_t[:, i, 1, a], ACT.Exp, scale=-0.5).then_inc(root_ready, 1)

            def attention_norm(n, b, in_batch=range(JB)):
                i, a = norm_order[n - 1]
                act.wait_ge(shift_ready, n - 2)
                for j in (a.start + t for t in in_batch):
                    rows_psum = bank[ATT_BANKS[2 * b][(j % JB) // 2]][:, (j % 2) * D:(j % 2 + 1) * D]
                    act.activation(rows[:, j, 0:D], rows_psum, ACT.Identity, bias=ln_t[:, i, 6, j:j + 1],
                                   scale=ln_t[:, i, 5, j:j + 1]).then_inc(att_ready, 1)

            def normalise(n):
                i, a = norm_order[n - 1]
                act.wait_ge(shift_ready, n - 2)
                for j in (j for j in range(a.start, a.stop) if j // 2 not in XN_DVE):
                    act.activation(rows[:, j, 0:D], x_tok[:, j], ACT.Identity, bias=ln_t[:, i, 6, j:j + 1],
                                   scale=ln_t[:, i, 5, j:j + 1]).then_inc(xn_ready, 1)

            def logits_bias(b):
                act.wait_ge(logits_t_psum, b + 1)
                act.activation(logits_t[:, b * S:(b + 1) * S], bank[6 + b][0:E, :], ACT.Identity, bias=r_bias
                               ).then_inc(logits_t_ready, 1)

            pool_experts = taken_by(POOL)

            def split_hi(first, last):
                for n in pool_experts[first:last]:
                    act.wait_ge(stage_in[plan[n][0]], 16 * fills(n))
                    act.activation(w_hi[:, expert_at(n)], stages[plan[n][0]], ACT.Copy).then_inc(w_hi_act, 1)

            def affine(b):
                for c in range(C):
                    act.wait_ge(hT_psum, b * C + c + 1)
                    act.activation(h_feat[:, c, b * S:(b + 1) * S], bank[ATT_BANKS[b][c]][:], ACT.Identity,
                                   bias=b_col[:, c:c + 1], scale=g_col[:, c:c + 1]).then_inc(hT_ready, 1)

            def query(b):
                for c in range(C):
                    act.wait_ge(q_psum, b * C + c + 1)
                    act.activation(q_feat[:, c, b * S:(b + 1) * S], bank[ATT_BANKS[2 + b][c]][:], ACT.Identity,
                                   bias=bq[:, c:c + 1]).then_inc(q_ready, 1)

            def exps(which, b, pair, psum_ready):
                for c in range(C):
                    act.wait_ge(psum_ready, b * C + c + 1)
                    if which:
                        act.wait_ge(eq_ready, b * C + c + 1)
                    act.activation(e_feat[:, c, b * S:(b + 1) * S], bank[ATT_BANKS[pair][c]][:], ACT.Exp,
                                   bias=bias_s[:, which, c:c + 1], scale=SCALE).then_inc(e_ready, 1)

            def inverse(which, b):
                for c in range(C):
                    n = which * U + b * C + c
                    unit = s_feat[:, c, b * S:(b + 1) * S]
                    act.wait_ge(sum_ready, n + 1)
                    act.activation(unit, unit, ACT.Ln).then_inc(log_ready, 1)
                for c in range(C):
                    n = which * U + b * C + c
                    unit = s_feat[:, c, b * S:(b + 1) * S]
                    act.wait_ge(log_ready, n + 1)
                    act.activation(unit, unit, ACT.Exp, scale=-1.0).then_inc(inv_ready, 1)

            def hi(p, i=0):
                u, par = p % RING, p % 2
                act.wait_ge(t_done, i + p + 1)
                if p >= RING:
                    act.wait_ge(gu_done, i + p - RING + 1)
                act.activation(xh[:, u].rearrange("p t c s -> p (t c s)"), bank[2 + par][:], ACT.Copy).then_inc(hi_done, 1)

            def silu(p, i=0):
                par = p % 2
                act.wait_ge(gu_done, i + p + 1)
                if p >= 2:
                    act.wait_ge(act_done, i + p - 1)
                act.activation(silu_t[:, par], bank[4 + par][:].rearrange("p (t g) -> p t g", t=2)[:, :, 0:P],
                               ACT.Silu).then_inc(silu_done, 1)

            def act_hi(p, i=0):
                par = p % 2
                act.wait_ge(a_done, i + p + 1)
                if p >= 2:
                    act.wait_ge(d_done, i + p - 1)
                act.activation(ah[:, par].rearrange("p t s -> p (t s)"), bank[6 + par][:, 0:2 * P], ACT.Copy).then_inc(ah_done, 1)

            def y_odd(p, i=0):
                if p % 2 == 0:
                    return
                u = p % RING
                act.wait_ge(d_done, i + p + 1)
                if p < SP_PAIRS:
                    act.activation(y_shared[:, 2 * p:2 * p + 2].rearrange("p t d -> p (t d)"), bank[1][:], ACT.Copy).then_inc(y_done[1], 1)
                    return
                if p >= FIRST + RING:
                    act.wait_ge(y_out[u], 16 * ((p - FIRST) // RING) + i * (16 // RING))
                act.activation(y_tiles[:, u].rearrange("p t d -> p (t d)"), bank[1][:], ACT.Copy).then_inc(y_done[1], 1)

            act.wait_ge(col_in, 16)
            roots(1)
            affine(0)
            roots(2)
            split_hi(0, 2)
            query(0)
            affine(1)
            act.wait_ge(bias_ready, 2)
            exps(0, 0, 0, qa_psum)
            split_hi(2, 3)
            inverse(0, 0)
            split_hi(3, 4)
            query(1)
            split_hi(4, 5)
            exps(0, 1, 2, qa_psum)
            split_hi(5, 6)
            inverse(0, 1)
            split_hi(6, 8)
            exps(1, 0, 0, ka_psum)
            inverse(1, 0)
            split_hi(8, 9)
            exps(1, 1, 1, ka_psum)
            split_hi(9, 10)
            inverse(1, 1)
            split_hi(10, NX)
            roots(3)
            act.wait_ge(w_lo_pool, NX - N_DVE)
            act.wait_ge(w_lo_dve, N_DVE)
            attention_norm(3, 0, range(0, JB // 2))
            roots(4)
            attention_norm(3, 0, range(JB // 2, JB))
            attention_norm(4, 1)
            roots(5)
            normalise(5)
            roots(6)
            hi(0)
            hi(1)
            normalise(6)
            hi(2)
            hi(3)
            logits_bias(0)
            logits_bias(1)
            silu(0)
            silu(1)
            act.wait_ge(tile_hot_ready, 1)
            act.activation(tile_lo, tile_hot, ACT.Copy, scale=tok_lo).then_inc(tile_lo_ready, 1)
            act_hi(0)
            silu(2)
            silu(3)
            act_hi(1)
            act_hi(2)
            y_odd(1)
            hi(FIRST)

            def step(p, i=0):
                if FIRST <= p < PAIRS:
                    silu(p, i)
                if FIRST <= p < PAIRS + 1:
                    act_hi(p - 1, i)
                if p + 2 < PAIRS or not isinstance(i, int):
                    hi(p + 2, i)
                if FIRST <= p < PAIRS + 2:
                    y_odd(p - 2, i)

            routed_steps(act, STEPS_BEFORE, step, STEPS_AFTER)
            act.preload_act_table_set("natural_log_exp_and_others")
            act.wait_ge(logits_ready, 2)
            act.activation(exp_e, diff_e, ACT.Exp).then_inc(exp_ready, 1)
            act.activation(rs[:, 4], rs[:, 6], ACT.Exp).then_inc(exp_ready, 1)
            for o in range(len(OUT_GROUPS)):
                i, a = norm_order[6 + o]
                roots(7 + o)
                act.wait_ge(shift_ready, 5 + o)
                for j in range(a.start, min(a.stop, NJ - 1)):
                    act.activation(total[:, j], total[:, j], ACT.Identity, bias=ln_t[:, i, 6, j:j + 1],
                                   scale=ln_t[:, i, 5, j:j + 1]).then_inc(out_normed, 1)

        @block.vector
        def _(v):
            steps = [0]

            def chain(ins):
                steps[0] += 1
                ins.then_inc(v_chain, 1)
                v.wait_ge(v_chain, steps[0])

            def statistics(n, srcs, scale, eps, ready=()):
                i, a = norm_order[n - 1]
                for t, src in enumerate(srcs):
                    if ready:
                        v.wait_ge(*ready[t])
                    last = v.bn_stats(stats[:, a.start + t, :], src)
                chain(last)
                finish_statistics(n, scale, eps)

            def finish_statistics(n, scale, eps):
                i, a = norm_order[n - 1]
                for j in range(a.start, a.stop):
                    last = v.bn_aggr(mv[:, i, j, :], stats[:, j, :])
                chain(last)
                v.tensor_scalar(ln_t[:, i, 0, a], mv[:, i, a, 1], scale, eps, ALU.mult, ALU.add).then_inc(var_ready, 1)

            def refine(n, want_shift=False):
                i, a = norm_order[n - 1]
                v.wait_ge(root_ready, n)
                chain(v.tensor_tensor(ln_t[:, i, 3, a], ln_t[:, i, 2, a], ln_t[:, i, 2, a], ALU.mult))
                chain(v.scalar_tensor_tensor(ln_t[:, i, 4, a], ln_t[:, i, 3, a], -0.5, ln_t[:, i, 0, a], ALU.mult, ALU.mult))
                chain(v.scalar_tensor_tensor(ln_t[:, i, 5, a], ln_t[:, i, 4, a], 1.5, ln_t[:, i, 2, a], ALU.add, ALU.mult))
                if want_shift:
                    v.scalar_tensor_tensor(ln_t[:, i, 6, a], mv[:, i, a, 0], -1.0, ln_t[:, i, 5, a], ALU.mult, ALU.mult).then_inc(shift_ready, 1)

            def normalise(n, src, dst, ready, pairs=range(NJ // 2)):
                i, a = norm_order[n - 1]
                for j in (j for j in range(a.start, a.stop) if j // 2 in pairs):
                    v.tensor_scalar(dst[:, j, 0:D], src[:, j], mv[:, i, j, 0:1], ln_t[:, i, 5, j:j + 1],
                                    ALU.subtract, ALU.mult).then_inc(ready, 1)

            for b in range(B):
                statistics(b + 1, [x_tok[:, j] for j in range(b * JB, (b + 1) * JB)], 1.0 + LN_EPS, LN_EPS * LN_EPS,
                           [(x_in[2 * b + h], 16) for h in range(2) for _ in range(JB // 2)])
                refine(b + 1)
                normalise(b + 1, x_tok, rows, hat_ready)
            v.wait_ge(col_in, 16)
            v.tensor_scalar(bias_s[:, 0], bqa, SCALE, None, ALU.mult).then_inc(bias_ready, 1)
            v.tensor_scalar(bias_s[:, 1], bka, SCALE, None, ALU.mult).then_inc(bias_ready, 1)

            v.tensor_copy(r_hi[:], wr).then_inc(r_split, 1)
            v.wait_ge(r_split, 1)
            v.tensor_tensor(r_lo[:], wr, r_hi[:].bitcast(F32), ALU.subtract).then_inc(r_split, 1)

            def split(first, last):
                for n in taken_by(DVE)[first:last]:
                    e = expert_at(n)
                    v.wait_ge(stage_in[plan[n][0]], 16 * fills(n))
                    chain(v.tensor_copy(w_hi[:, e], stages[plan[n][0]]))
                    v.tensor_tensor(w_lo[:, e], stages[plan[n][0]], w_hi[:, e].bitcast(F32), ALU.subtract).then_inc(w_lo_dve, 1)

            def cumulate(which, b):
                for c in range(C):
                    n = which * U + b * C + c
                    a = slice(b * S, (b + 1) * S)
                    v.wait_ge(e_ready, n + 1)
                    v.tensor_tensor_scan(s_feat[:, c, a], e_feat[:, c, a], e_feat[:, c, a], 0.0, ALU.add, ALU.bypass).then_inc(sum_ready, 1)

            def pool_query(b, pair):
                a = slice(b * S, (b + 1) * S)
                for c in range(C):
                    n = b * C + c
                    v.wait_ge(inv_ready, n + 1)
                    v.wait_ge(eq_ready, n + 1)
                    chain(v.tensor_tensor(s_feat[:, c, a], q_feat[:, c, a], s_feat[:, c, a], ALU.mult))
                    chain(v.tensor_tensor_scan(p_feat[:, c, a], s_feat[:, c, a], s_feat[:, c, a], 0.0, ALU.add, ALU.bypass))
                    v.wait_ge(k_psum, n + 1)
                    v.scalar_tensor_tensor(m_feat[:, c, a], bank[ATT_BANKS[pair][c]][:], bk[:, c:c + 1], p_feat[:, c, a],
                                           ALU.add, ALU.mult).then_inc(mix_ready, 1)

            def pool_keys(b):
                a = slice(b * S, (b + 1) * S)
                for c in range(C):
                    n = b * C + c
                    v.wait_ge(inv_ready, U + n + 1)
                    v.wait_ge(eq_ready, U + n + 1)
                    chain(v.tensor_tensor(s_feat[:, c, a], m_feat[:, c, a], s_feat[:, c, a], ALU.mult))
                    chain(v.tensor_tensor_scan(p_feat[:, c, a], s_feat[:, c, a], s_feat[:, c, a], 0.0, ALU.add, ALU.bypass))

            def values(b, pair):
                a = slice(b * S, (b + 1) * S)
                for c in range(C):
                    v.wait_ge(v_psum, b * C + c + 1)
                    v.scalar_tensor_tensor(e_feat[:, c, a], bank[ATT_BANKS[pair][c]][:], bv[:, c:c + 1], p_feat[:, c, a],
                                           ALU.add, ALU.mult).then_inc(a_ready, 1)

            def att_rows(b, j):
                return bank[ATT_BANKS[2 * b][j // 2]][:, (j % 2) * D:(j % 2 + 1) * D]

            def att_statistics(b, half):
                v.wait_ge(aT_psum, 2 * b + half + 1)
                for j in range(half * JB // 2, (half + 1) * JB // 2):
                    last = v.bn_stats(stats[:, b * JB + j, :], att_rows(b, j))
                return last

            def add_x():
                v.wait_ge(att_ready, X1_DVE + 1)
                v.tensor_tensor(x_tok[:, X1_DVE], rows[:, X1_DVE], x_tok[:, X1_DVE], ALU.add).then_inc(x1_dve, 1)

            def x1_statistics(j):
                if j == X1_DVE:
                    v.wait_ge(x1_dve, 1)
                else:
                    v.wait_ge(x1_ready, j + (j < X1_DVE))
                return v.bn_stats(stats[:, j, :], x_tok[:, j])

            def lo(p, i=0):
                u, par = p % RING, p % 2
                v.wait_ge(hi_done, i + p + 1)
                v.tensor_tensor(xl[:, u].rearrange("p t c s -> p (t c s)"), bank[2 + par][:],
                                xh[:, u].rearrange("p t c s -> p (t c s)").bitcast(F32), ALU.subtract).then_inc(lo_done, 1)
            def gated(p, i=0):
                par = p % 2
                v.wait_ge(silu_done, i + p + 1)
                if p >= 2:
                    v.wait_ge(a_done, i + p - 1)
                v.tensor_tensor(act_t[:, par], silu_t[:, par], bank[4 + par][:].rearrange("p (t g) -> p t g", t=2)[:, :, P:GU],
                                ALU.mult).then_inc(act_done, 1)

            def act_lo(p, i=0):
                par = p % 2
                v.wait_ge(ah_done, i + p + 1)
                v.tensor_tensor(al[:, par].rearrange("p t s -> p (t s)"), bank[6 + par][:, 0:2 * P],
                                ah[:, par].rearrange("p t s -> p (t s)").bitcast(F32), ALU.subtract).then_inc(al_done, 1)

            def y_even(p, i=0):
                if p % 2:
                    return
                u = p % RING
                v.wait_ge(d_done, i + p + 1)
                if p < SP_PAIRS:
                    v.tensor_copy(y_shared[:, 2 * p:2 * p + 2].rearrange("p t d -> p (t d)"), bank[0][:]).then_inc(y_done[0], 1)
                    return
                if p >= FIRST + RING:
                    v.wait_ge(y_out[u], 16 * ((p - FIRST) // RING) + i * (16 // RING))
                v.tensor_copy(y_tiles[:, u].rearrange("p t d -> p (t d)"), bank[0][:]).then_inc(y_done[0], 1)

            split(0, 3)
            cumulate(0, 0)
            pool_query(0, 1)
            split(3, 4)
            cumulate(0, 1)
            pool_query(1, 3)
            cumulate(1, 0)
            split(4, 5)
            pool_keys(0)
            cumulate(1, 1)
            values(0, 2)
            pool_keys(1)
            values(1, 3)
            att_statistics(0, 0)
            chain(att_statistics(0, 1))
            finish_statistics(3, 1.0, LN_EPS)
            att_statistics(1, 0)
            refine(3, True)
            chain(att_statistics(1, 1))
            finish_statistics(4, 1.0, LN_EPS)
            refine(4, True)
            for j in range(JB - 1):
                x1_statistics(j)
                if j == JB - 3:
                    add_x()
            chain(x1_statistics(JB - 1))
            finish_statistics(5, 1.0, LN_EPS)
            for j in range(JB, JB + 2):
                x1_statistics(j)
            refine(5, True)
            x1_statistics(NJ - 2)
            chain(x1_statistics(NJ - 1))
            finish_statistics(6, 1.0, LN_EPS)
            normalise(5, x_tok, rows, xn_dve, XN_DVE)
            refine(6, True)
            normalise(6, x_tok, rows, xn_dve, XN_DVE)
            for p in range(SP_PAIRS):
                lo(p)

            def over_e(a):
                return a.rearrange("p (j o) -> p j o", o=1).to_broadcast([P, NJ, E])

            def over_j(a):
                return a.rearrange("p (o e) -> p o e", o=1).to_broadcast([P, NJ, E])

            v.wait_ge(logits_psum, B)
            logits = bank[0][:, 0:NJ * E].rearrange("p (j e) -> p j e", e=E)
            chain(v.tensor_reduce(rs[:, 0], logits, AX_X, ALU.max))
            chain(v.tensor_tensor(rt[:, 3], logits, over_e(rs[:, 0]), ALU.is_equal))
            chosen_k = rt[:, 8:10]
            for k in range(K):
                if k:
                    chain(v.scalar_tensor_tensor(rt[:, 5], chosen_k[:, 0], -3.0e38, logits, ALU.mult, ALU.add))
                    chain(v.tensor_reduce(rs[:, 3], rt[:, 5], AX_X, ALU.max))
                    chain(v.tensor_tensor(rt[:, 3], rt[:, 5], over_e(rs[:, 3]), ALU.is_equal))
                chain(v.tensor_tensor(rt[:, 4], rt[:, 3], over_j(rev_e), ALU.mult))
                chain(v.tensor_reduce(rs[:, 1 + k], rt[:, 4], AX_X, ALU.max))
                chain(v.tensor_tensor(chosen_k[:, k], rt[:, 4], over_e(rs[:, 1 + k]), ALU.is_equal))
            v.tensor_tensor(chosen[:], chosen_k[:, 0], chosen_k[:, 1], ALU.add).then_inc(chosen_ready, 1)
            v.tensor_tensor(diff_e, logits, over_e(rs[:, 0]), ALU.subtract).then_inc(logits_ready, 1)
            v.tensor_tensor(rs[:, 6], rs[:, 3], rs[:, 0], ALU.subtract).then_inc(logits_ready, 1)
            chain(v.memset(before[:, 0:1], 0.0))
            gated(0)
            v.wait_ge(rank_psum, 2)
            chain(v.tensor_scalar(ex[:, 0], bank[7][:, 256:256 + E], 1.0 / P, 0.5 - 0.5 / P, ALU.mult, ALU.add))
            chain(v.tensor_scalar(ex[:, 1], ex[:, 0], ROUND, -ROUND, ALU.add, ALU.add))
            chain(v.tensor_tensor_scan(before[:, 1:], ex[:, 1], ex[:, 1], 0.0, ALU.add, ALU.bypass))
            chain(v.scalar_tensor_tensor(rt[:, 10], over_j(before[:, 0:E]), float(P),
                                         bank[1][:, 0:NJ * E].rearrange("p (j e) -> p j e", e=E), ALU.mult, ALU.add))
            chain(v.tensor_tensor(rt[:, 6:8], chosen_k, rt[:, 10:11].to_broadcast([P, K, NJ, E]), ALU.mult))
            chain(v.tensor_reduce(rs[:, 8:10], rt[:, 6:8], AX_X, ALU.add))
            slot, tile_f, pos = (rs[:, n:n + 2].rearrange("p k j -> p (k j)") for n in (8, 12, 14))
            chain(v.tensor_scalar(rs[:, 10:12].rearrange("p k j -> p (k j)"), slot, 1.0 / P, 0.5 / P - 0.5, ALU.mult, ALU.add))
            chain(v.tensor_scalar(tile_f, rs[:, 10:12].rearrange("p k j -> p (k j)"), ROUND, -ROUND, ALU.add, ALU.add))
            v.tensor_tensor(tile_hot, tile_f.rearrange("p (n o) -> p n o", o=1).to_broadcast([P, KJ, TILES]),
                            tile_no.rearrange("p (o m) -> p o m", o=1).to_broadcast([P, KJ, TILES]), ALU.is_equal
                            ).then_inc(tile_hot_ready, 1)
            chain(v.scalar_tensor_tensor(pos, tile_f, -float(P), slot, ALU.mult, ALU.add))
            v.wait_ge(w_lo_pool, NX - N_DVE)
            for n in range(KJ):
                v.tensor_scalar(pos_hot[:, n], pos_no[:], pos[:, n:n + 1], None, ALU.is_equal).then_inc(pos_hot_ready, 1)
            v.tensor_copy(slot_of[:].rearrange("p k j -> p (k j)"), slot).then_inc(slot_ready, 1)
            gated(1)
            v.wait_ge(token_psum, 1)
            v.tensor_copy(token_of[:], bank[1][:, 256:256 + TILES]).then_inc(token_ready, 1)
            gated(2)
            act_lo(0)
            gated(3)
            act_lo(1)
            chain(v.tensor_tensor(cmp[:], before[:, 1:].rearrange("p (o e) -> p o e", o=1).to_broadcast([P, TILES, E]),
                                  tile_no.rearrange("p (m o) -> p m o", o=1).to_broadcast([P, TILES, E]), ALU.is_le))
            chain(v.tensor_reduce(tile_e[:, 0], cmp[:], AX_X, ALU.add))
            v.tensor_scalar(tile_e_i[:], tile_e[0:1, 0], float(E - 1), None, ALU.min).then_inc(tile_e_ready, 1)
            y_even(0)
            act_lo(2)
            lo(FIRST)

            def step(p, i=0):
                if FIRST <= p < PAIRS:
                    gated(p, i)
                if FIRST <= p < PAIRS + 1:
                    act_lo(p - 1, i)
                if p + 2 < PAIRS or not isinstance(i, int):
                    lo(p + 2, i)
                if FIRST <= p < PAIRS + 2:
                    y_even(p - 2, i)

            routed_steps(v, STEPS_BEFORE, step, STEPS_AFTER)

            v.wait_ge(exp_ready, 2)
            chain(v.tensor_reduce(rs[:, 5], exp_e, AX_X, ALU.add))
            chain(v.scalar_tensor_tensor(rs[:, 6], rs[:, 5], TOPK_EPS, rs[:, 4], ALU.mult, ALU.add))
            chain(v.tensor_scalar(rs[:, 7], rs[:, 6], 1.0, None, ALU.add))
            chain(v.reciprocal(gate_w[:, 0], rs[:, 7]))
            v.tensor_tensor(gate_w[:, 1], gate_w[:, 0], rs[:, 4], ALU.mult).then_inc(gates_ready, 1)
            v.wait_ge(gates_ready, 1)
            v.wait_ge(y_done[1], PAIRS // 2)

            def sum_statistics(j):
                v.wait_ge(total_ready, j + 1)
                return v.bn_stats(stats[:, j, :], total[:, j])

            for o, a in enumerate(OUT_GROUPS):
                for j in range(a.start, a.stop):
                    v.wait_ge(yc_in[0][j], 16)
                    v.scalar_tensor_tensor(total[:, j], y_choice[0][:, j], gate_w[:, 0, j:j + 1], y_shared[:, j],
                                           ALU.mult, ALU.add).then_inc(first_added, 1)
                    if j > a.start:
                        sum_statistics(j - 1)
                    if j == OUT_GROUPS[1].start:
                        add_x1(v, 0)
                    v.wait_ge(first_added, j + 1)
                    v.wait_ge(yc_in[1][j], 16)
                    v.scalar_tensor_tensor(total[:, j], y_choice[1][:, j], gate_w[:, 1, j:j + 1], total[:, j],
                                           ALU.mult, ALU.add).then_inc(total_ready, 1)
                    if j == OUT_GROUPS[-1].start:
                        refine(7 + o - 1, True)
                chain(sum_statistics(a.stop - 1))
                finish_statistics(7 + o, 1.0, LN_EPS)
                if o != len(OUT_GROUPS) - 2:
                    refine(7 + o, True)
            i, j = N_OUT, NJ - 1
            v.tensor_scalar(total[:, j], total[:, j], mv[:, i, j, 0:1], ln_t[:, i, 5, j:j + 1],
                            ALU.subtract, ALU.mult).then_inc(last_normed, 1)
            add_x1(v, len(OUT_GROUPS) - 1)

        @block.gpsimd
        def _(g):
            g.memset(ident[:], 0.0).then_inc(consts, 1)
            g.memset(earlier[:], 1.0).then_inc(consts, 1)
            g.memset(ones_bf[:], 1.0).then_inc(consts, 1)
            g.wait_ge(consts, 3)
            g.affine_select(out=ident[:], in_=ident[:], compare_op=ALU.not_equal, fill=1.0, base=0,
                            pattern=[[-1, P]], channel_multiplier=1).then_inc(consts2, 1)
            g.affine_select(out=earlier[:], in_=earlier[:], compare_op=ALU.is_gt, fill=0.0, base=0,
                            pattern=[[1, P]], channel_multiplier=-1).then_inc(consts2, 1)
            g.iota(idx_i[:, 0:E], [[-1, E]], base=E, channel_multiplier=0).then_inc(consts, 1)
            g.iota(idx_i[:, E:E + TILES], [[1, TILES]], base=0, channel_multiplier=0).then_inc(consts, 1)
            g.iota(idx_i[:, E + TILES:E + TILES + P], [[1, P]], base=0, channel_multiplier=0).then_inc(consts, 1)
            g.iota(idx_i[:, E + TILES + P:N_IDX - 1], [[0, K], [P, NJ]], base=0, channel_multiplier=0).then_inc(consts, 1)
            g.iota(idx_i[:, N_IDX - 1:], [[1, 1]], base=0, channel_multiplier=1).then_inc(consts, 1)
            g.wait_ge(consts, 8)
            g.tensor_copy(idx_f[:], idx_i[:]).then_inc(consts2, 1)
            g.tensor_copy(pos_no[:], idx_i[:, E + TILES:E + TILES + P]).then_inc(consts2, 1)

            pool_experts = taken_by(POOL)

            def split_lo(first, last):
                for i, n in list(enumerate(pool_experts))[first:last]:
                    e = expert_at(n)
                    g.wait_ge(w_hi_act, i + 1)
                    g.tensor_tensor(w_lo[:, e], stages[plan[n][0]], w_hi[:, e].bitcast(F32), ALU.subtract).then_inc(w_lo_pool, 1)

            def weighted(which, b):
                src = m_feat if which else q_feat
                for c in range(C):
                    a = slice(b * S, (b + 1) * S)
                    g.wait_ge(e_ready, which * U + b * C + c + 1)
                    if not which:
                        g.wait_ge(qa_psum, (b + 1) * C)
                    else:
                        g.wait_ge(ka_psum, (b + 1) * C)
                    g.tensor_tensor(src[:, c, a], e_feat[:, c, a], src[:, c, a], ALU.mult).then_inc(eq_ready, 1)

            split_lo(0, 2)
            weighted(0, 0)
            split_lo(2, 5)
            weighted(0, 1)
            split_lo(5, 8)
            weighted(1, 0)
            split_lo(8, 9)
            weighted(1, 1)
            split_lo(9, NX)
            for j in range(NJ):
                if j == X1_DVE:
                    continue
                g.wait_ge(att_ready, j + 1)
                g.tensor_tensor(x_tok[:, j], rows[:, j, 0:D], x_tok[:, j], ALU.add).then_inc(x1_ready, 1)
            g.wait_ge(w_lo_pool, NX - N_DVE)
            g.wait_ge(w_lo_dve, N_DVE)
            g.wait_ge(tile_hot_ready, 1)
            g.tensor_tensor(tile_hi, tile_hot, tok_hi.rearrange("p (n o) -> p n o", o=1).to_broadcast([P, KJ, TILES]),
                            ALU.mult).then_inc(tile_hi_ready, 1)
            g.wait_ge(normed_out, 16 * B)
            g.wait_ge(token_ready, 1)
            for p in range(FIRST, PAIRS):
                if p >= FIRST + RING:
                    g.wait_ge(t_done, p - RING + 1)
                for t in range(2):
                    m = (p - FIRST) * 2 + t
                    g.indirect_dma_start(out=x_tiles[:, p % RING, t], out_offset=None, in_=normed,
                                         in_offset=bass.IndirectOffsetOnAxis(token_of[:, m:m + 1], 0)
                                         ).then_inc(xt_in[p % RING], 16)
            g.wait_ge(slot_ready, 1)
            for u in range(RING):
                g.wait_ge(y_out[u], 16 * (PAIRS - FIRST) // RING)
            for j in range(NJ):
                for k in range(K):
                    g.indirect_dma_start(out=y_choice[k][:, j], out_offset=None, in_=y_slots,
                                         in_offset=bass.IndirectOffsetOnAxis(slot_of[:, k, j:j + 1], 0)
                                         ).then_inc(yc_in[k][j], 16)
            add_x1(g, POOL_GROUP)


def kernel(**inputs):
    import numpy as np
    import concourse.bacc as bacc
    from concourse.bass_utils import run_bass_kernel_spmd

    a = {n: np.asarray(v) for n, v in inputs.items()}
    x = np.ascontiguousarray(a["L0_attn_hidden_states"])
    D = x.shape[2]
    C = D // P
    attn_w = np.stack([a["L0_attn_" + n].T.reshape(C, P, D) for n in ("Wq", "Wqa", "Wk", "Wka", "Wv")])
    attn_w = np.ascontiguousarray(attn_w.transpose(2, 0, 1, 3))
    cols = np.stack([a["L0_attn_" + n].reshape(C, P) for n in ("ln_g", "ln_b", "bq", "bqa", "bk", "bka", "bv")])
    wr = a["L0_ffn_Wr"].T.reshape(C, P, -1)
    E = wr.shape[2]
    bias = np.zeros((P, 1), x.dtype)
    bias[:E, 0] = a["L0_ffn_bias"].reshape(-1)
    misc = np.concatenate([cols.transpose(2, 0, 1).reshape(P, -1), wr.transpose(1, 0, 2).reshape(P, -1),
                           bias], axis=1)
    misc = np.ascontiguousarray(misc)
    wg = np.concatenate([a["L0_ffn_Wg"], a["L0_ffn_sWg"][None]])
    wu = np.concatenate([a["L0_ffn_Wu"], a["L0_ffn_sWu"][None]])
    wd = np.concatenate([a["L0_ffn_Wd"], a["L0_ffn_sWd"][None]])
    gu = np.concatenate([wg, wu], axis=2).reshape(E + 1, C, P, -1).transpose(2, 0, 1, 3).reshape(P, E + 1, -1)
    expert_w = np.ascontiguousarray(np.concatenate([gu, wd.transpose(1, 0, 2)], axis=2))

    nc = bacc.Bacc("TRN2", target_bir_lowering=False, num_devices=1)
    arrays = {"x": x, "attn_w": attn_w, "misc": misc, "expert_w": expert_w}
    args = [nc.dram_tensor(n, v.shape, mybir.dt.from_np(v.dtype), kind="ExternalInput").ap() for n, v in arrays.items()]
    out = nc.dram_tensor("out", x.shape, F32, kind="ExternalOutput").ap()
    block_kernel(nc, *args, out)
    r = run_bass_kernel_spmd(nc, [arrays], core_ids=[0])
    return r.results[0]["out"]
```
